# Optimizing a Trainium2 kernel written in Bass

```python
import numpy as np
import jax
import jax.numpy as jnp

def _softmax(x, axis=-1):
    return jax.nn.softmax(x, axis=axis)

def _gelu(x):
    return jax.nn.gelu(x, approximate=True)

def _silu(x):
    return jax.nn.silu(x)

def _sigmoid(x):
    return jax.nn.sigmoid(x)

def _layernorm(x, axis=-1, eps=1e-05):
    m = jnp.mean(x, axis=axis, keepdims=True)
    v = jnp.var(x, axis=axis, keepdims=True)
    return (x - m) / jnp.sqrt(v + eps)

def _scatter_add(tgt, idx, src, axis=0):
    return tgt.at[idx].add(src)

def _segment_sum(src, seg, n):
    return jax.ops.segment_sum(src, seg, n)
kernel_name = 'mk_decoder_preln_d1_seqx_r4_27d2e2'

def setup_inputs(seed: int=0):
    np.random.seed(seed)
    _w = jnp.asarray

    def _rec_inputs():
        import jax
        import jax.numpy as jnp
        _rk = jax.random.key(seed)
        x = -0.0002928 + 1 * jax.random.normal(jax.random.fold_in(_rk, 1), (16, 256, 256), jnp.float32)
        _lenS = 256 - jax.random.randint(jax.random.fold_in(_rk, 7), (16,), 0, max(1, 256 // 4) + 1, jnp.int32)
        _lenS2 = 256 - jax.random.randint(jax.random.fold_in(_rk, 8), (16,), 0, max(1, 256 // 4) + 1, jnp.int32)
        _ctx_1024P = jax.random.normal(jax.random.fold_in(_rk, 11), (16, 16, 256), jnp.float32)
        _ctx_1024c = jax.random.dirichlet(jax.random.fold_in(_rk, 511), 0.3 * jnp.ones((16,), jnp.float32), (16, 256))
        _ctx_1024t = jnp.einsum('bsk,bkd->bsd', _ctx_1024c, _ctx_1024P)
        _ctx_1024t = _ctx_1024t * jax.lax.rsqrt(jnp.mean(jnp.square(_ctx_1024t)) + 1e-12) * 0.953939
        ctx_1024 = -1.39393e-06 + 0.999914 * (_ctx_1024t + 0.3 * jax.random.normal(jax.random.fold_in(_rk, 611), (16, 256, 256), jnp.float32))
        _validS = jnp.arange(256)[None, :] < _lenS[:, None]
        _validS2 = jnp.arange(256)[None, :] < _lenS2[:, None]
        _causal = jnp.tril(jnp.ones((256, 256), dtype=bool))
        mask_1x1xSxS2_ik0 = jnp.where(jnp.broadcast_to(_validS2[0:1, None, None, :], (1, 1, 256, 256)), 0, 1).astype(jnp.int32)
        return (x, ctx_1024, mask_1x1xSxS2_ik0)
    x, ctx_1024, mask_1x1xSxS2_ik0 = _rec_inputs()

    def _L0_attn_setup():
        import jax, jax.numpy as jnp
        import numpy as np
        B, T, D = (4, 512, 256)
        key = jax.random.key(seed)
        kx, kq, kk, kv = jax.random.split(key, 4)
        scale = 1.0 / np.sqrt(D)
        return {'x': jax.random.normal(kx, (B, T, D), dtype=jnp.float32), 'Wq': jax.random.normal(kq, (D, D), dtype=jnp.float32) * scale, 'Wk': jax.random.normal(kk, (D, D), dtype=jnp.float32) * scale, 'Wv': jax.random.normal(kv, (D, D), dtype=jnp.float32) * scale}
    _L0_attn_all = _L0_attn_setup()
    _L0_attn_in = {k: v for k, v in _L0_attn_all.items() if k in ('Wq', 'Wk', 'Wv')}
    del _L0_attn_all

    def _L0_xattn_setup():
        import jax, jax.numpy as jnp
        import numpy as np
        B, S, D, H = (2, 512, 256, 16)
        DK = D // H

        def rope_tables(seq_len, d_k):
            inv_freq = 1.0 / 10000.0 ** (jnp.arange(0, d_k, 2, dtype=jnp.float32) / d_k)
            t = jnp.arange(seq_len, dtype=jnp.float32)
            freqs = jnp.einsum('i,j->ij', t, inv_freq)
            emb = jnp.concatenate([freqs, freqs], axis=-1)
            return (jnp.cos(emb), jnp.sin(emb))

        def apply_rope(x, cos, sin):
            b, h, s, dk = x.shape
            xr = x.reshape(b, h, s, dk // 2, 2)
            cr = cos.reshape(1, 1, s, dk // 2, 2)
            sr = sin.reshape(1, 1, s, dk // 2, 2)
            out = jnp.stack([xr[..., 0] * cr[..., 0] - xr[..., 1] * sr[..., 0], xr[..., 0] * sr[..., 1] + xr[..., 1] * cr[..., 1]], axis=-1)
            return out.reshape(b, h, s, dk)
        key = jax.random.key(seed)
        ks = jax.random.split(key, 7)
        scale = 1.0 / np.sqrt(D)
        q = jax.random.normal(ks[0], (B, S, D), dtype=jnp.float32)
        k = jax.random.normal(ks[1], (B, S, D), dtype=jnp.float32)
        v = jax.random.normal(ks[2], (B, S, D), dtype=jnp.float32)
        mask = jnp.tril(jnp.ones((S, S), dtype=jnp.int32))[None, None]
        wq = jax.random.normal(ks[3], (D, D), dtype=jnp.float32) * scale
        wk = jax.random.normal(ks[4], (D, D), dtype=jnp.float32) * scale
        wv = jax.random.normal(ks[5], (D, D), dtype=jnp.float32) * scale
        wo = jax.random.normal(ks[6], (D, D), dtype=jnp.float32) * scale
        return {'q': q, 'k': k, 'v': v, 'mask': mask, 'wq': wq, 'wk': wk, 'wv': wv, 'wo': wo}
    _L0_xattn_all = _L0_xattn_setup()
    _L0_xattn_in = {k: v for k, v in _L0_xattn_all.items() if k in ('wq', 'wk', 'wv', 'wo')}
    del _L0_xattn_all

    def _L0_ffn_setup():
        import jax, jax.numpy as jnp
        import numpy as np
        D_MODEL = 256
        D_FF = 1024
        N_EXPERTS = 8
        D_EXPERT = D_FF // N_EXPERTS
        TOP_K = 2
        LB_WEIGHT = 0.01
        B, S = (4, 512)

        def _top_k_softmax(logits, k):
            vals, _ = jax.lax.top_k(logits, k)
            thresh = vals[..., -1:]
            masked = jnp.where(logits >= thresh, logits, -jnp.inf)
            return jax.nn.softmax(masked, axis=-1)
        key = jax.random.key(seed)
        ks = jax.random.split(key, 8)
        x = jax.random.normal(ks[0], (B, S, D_MODEL), dtype=jnp.float32)
        w1 = jax.random.normal(ks[1], (N_EXPERTS, D_MODEL, D_EXPERT), dtype=jnp.float32) * (1.0 / np.sqrt(D_MODEL))
        b1 = jnp.zeros((N_EXPERTS, D_EXPERT), dtype=jnp.float32)
        w2 = jax.random.normal(ks[2], (N_EXPERTS, D_EXPERT, D_MODEL), dtype=jnp.float32) * (1.0 / np.sqrt(D_EXPERT))
        b2 = jnp.zeros((N_EXPERTS, D_MODEL), dtype=jnp.float32)
        centroids = jax.random.normal(ks[3], (N_EXPERTS, D_MODEL), dtype=jnp.float32) * 0.02
        w_route = jax.random.normal(ks[4], (N_EXPERTS, D_MODEL), dtype=jnp.float32) * (1.0 / np.sqrt(D_MODEL))
        return {'x': x, 'w1': w1, 'b1': b1, 'w2': w2, 'b2': b2, 'centroids': centroids, 'w_route': w_route}
    _L0_ffn_all = _L0_ffn_setup()
    _L0_ffn_in = {k: v for k, v in _L0_ffn_all.items() if k in ('w1', 'b1', 'w2', 'b2', 'centroids', 'w_route')}
    del _L0_ffn_all
    return {'x': x, 'ctx_1024': ctx_1024, 'mask_1x1xSxS2_ik0': mask_1x1xSxS2_ik0, 'L0_attn_Wq': _L0_attn_in['Wq'], 'L0_attn_Wk': _L0_attn_in['Wk'], 'L0_attn_Wv': _L0_attn_in['Wv'], 'L0_xattn_wq': _L0_xattn_in['wq'], 'L0_xattn_wk': _L0_xattn_in['wk'], 'L0_xattn_wv': _L0_xattn_in['wv'], 'L0_xattn_wo': _L0_xattn_in['wo'], 'L0_ffn_w1': _L0_ffn_in['w1'], 'L0_ffn_b1': _L0_ffn_in['b1'], 'L0_ffn_w2': _L0_ffn_in['w2'], 'L0_ffn_b2': _L0_ffn_in['b2'], 'L0_ffn_centroids': _L0_ffn_in['centroids'], 'L0_ffn_w_route': _L0_ffn_in['w_route']}

def reference(x, ctx_1024, mask_1x1xSxS2_ik0, L0_attn_Wq, L0_attn_Wk, L0_attn_Wv, L0_xattn_wq, L0_xattn_wk, L0_xattn_wv, L0_xattn_wo, L0_ffn_w1, L0_ffn_b1, L0_ffn_w2, L0_ffn_b2, L0_ffn_centroids, L0_ffn_w_route):
    import jax
    import jax.numpy as jnp

    def _L0_attn_ref(x, Wq, Wk, Wv):
        import jax, jax.numpy as jnp
        import numpy as np
        B, T, D = (4, 512, 256)
        q = jnp.einsum('btd,od->bto', x, Wq)
        k = jnp.einsum('btd,od->bto', x, Wk)
        v = jnp.einsum('btd,od->bto', x, Wv)
        scores = jnp.einsum('bqd,bkd->bqk', q, k)
        inv_sqrt_d = 1.0 / np.sqrt(k.shape[-1]).astype(np.float32)
        weights = jax.nn.softmax(scores * inv_sqrt_d, axis=-1)
        return jnp.einsum('bqk,bkd->bqd', weights, v)

    def _L0_xattn_ref(q, k, v, mask, wq, wk, wv, wo):
        import jax, jax.numpy as jnp
        import numpy as np
        B, S, D, H = (2, 512, 256, 16)
        DK = D // H

        def rope_tables(seq_len, d_k):
            inv_freq = 1.0 / 10000.0 ** (jnp.arange(0, d_k, 2, dtype=jnp.float32) / d_k)
            t = jnp.arange(seq_len, dtype=jnp.float32)
            freqs = jnp.einsum('i,j->ij', t, inv_freq)
            emb = jnp.concatenate([freqs, freqs], axis=-1)
            return (jnp.cos(emb), jnp.sin(emb))

        def apply_rope(x, cos, sin):
            b, h, s, dk = x.shape
            xr = x.reshape(b, h, s, dk // 2, 2)
            cr = cos.reshape(1, 1, s, dk // 2, 2)
            sr = sin.reshape(1, 1, s, dk // 2, 2)
            out = jnp.stack([xr[..., 0] * cr[..., 0] - xr[..., 1] * sr[..., 0], xr[..., 0] * sr[..., 1] + xr[..., 1] * cr[..., 1]], axis=-1)
            return out.reshape(b, h, s, dk)
        b, s, d = q.shape
        query = jnp.einsum('bsd,od->bso', q, wq).reshape(b, s, H, DK).transpose(0, 2, 1, 3)
        key_ = jnp.einsum('bsd,od->bso', k, wk).reshape(b, s, H, DK).transpose(0, 2, 1, 3)
        value = jnp.einsum('bsd,od->bso', v, wv).reshape(b, s, H, DK).transpose(0, 2, 1, 3)
        cos, sin = rope_tables(s, DK)
        query = apply_rope(query, cos, sin)
        key_ = apply_rope(key_, cos, sin)
        scores = jnp.einsum('bhqd,bhkd->bhqk', query, key_) / jnp.sqrt(jnp.float32(DK))
        scores = jnp.where(mask == 0, jnp.float32(-1000000000.0), scores)
        attn = jax.nn.softmax(scores, axis=-1)
        x = jnp.einsum('bhqk,bhkd->bhqd', attn, value)
        x = x.transpose(0, 2, 1, 3).reshape(b, s, H * DK)
        return jnp.einsum('bsd,od->bso', x, wo)

    def _L0_ffn_ref(x, w1, b1, w2, b2, centroids, w_route):
        import jax, jax.numpy as jnp
        import numpy as np
        D_MODEL = 256
        D_FF = 1024
        N_EXPERTS = 8
        D_EXPERT = D_FF // N_EXPERTS
        TOP_K = 2
        LB_WEIGHT = 0.01
        B, S = (4, 512)

        def _top_k_softmax(logits, k):
            vals, _ = jax.lax.top_k(logits, k)
            thresh = vals[..., -1:]
            masked = jnp.where(logits >= thresh, logits, -jnp.inf)
            return jax.nn.softmax(masked, axis=-1)
        eps = 1e-12
        x_norm = x / jnp.maximum(jnp.linalg.norm(x, axis=-1, keepdims=True), eps)
        c_norm = centroids / jnp.maximum(jnp.linalg.norm(centroids, axis=-1, keepdims=True), eps)
        cos_scores = jnp.einsum('bsd,ed->bse', x_norm, c_norm)
        route_scores = jnp.einsum('bsd,ed->bse', x, w_route)
        logits = cos_scores + route_scores
        gates = _top_k_softmax(logits, TOP_K)
        h = jax.nn.gelu(jnp.einsum('bsd,edh->bseh', x, w1) + b1, approximate=False)
        expert_out = jnp.einsum('bseh,ehd->bsed', h, w2) + b2
        out = jnp.einsum('bse,bsed->bsd', gates, expert_out)
        return out
    x = x + _L0_attn_ref(_layernorm(x, axis=-1), L0_attn_Wq, L0_attn_Wk, L0_attn_Wv)
    x = x + _L0_xattn_ref(_layernorm(x, axis=-1), ctx_1024, ctx_1024, mask_1x1xSxS2_ik0, L0_xattn_wq, L0_xattn_wk, L0_xattn_wv, L0_xattn_wo)
    x = x + _L0_ffn_ref(_layernorm(x, axis=-1), L0_ffn_w1, L0_ffn_b1, L0_ffn_w2, L0_ffn_b2, L0_ffn_centroids, L0_ffn_w_route)
    return x

_drawn_inputs = setup_inputs


def setup_inputs(seed=0):
    import zlib

    import numpy as np

    out = dict(_drawn_inputs(seed))
    spreads = {'L0_ffn_b1': (0.0, 0.1), 'L0_ffn_b2': (0.0, 0.1)}
    factors = {}
    for name, (base, spread) in spreads.items():
        noise = np.random.default_rng([zlib.crc32(name.encode()), seed]).standard_normal(out[name].shape)
        drawn = base * np.exp(spread * noise) if base else spread * noise
        out[name] = jnp.asarray(drawn.astype(out[name].dtype))
    for name, factor in factors.items():
        out[name] = (out[name] * factor).astype(out[name].dtype)
    return out
```

```python
from contextlib import ExitStack

import concourse.bass as bass
from concourse import mybir

ALU = mybir.AluOpType
ACT = mybir.ActivationFunctionType
AX_X = mybir.AxisListType.X
F32 = mybir.dt.float32
F32R = mybir.dt.float32r
BF16 = mybir.dt.bfloat16
I32 = mybir.dt.int32

P = 128
B = 16
S = 256
T = S // P
D = 256
C = D // P
H = 16
DK = D // H
HC = P // DK
E = 8
DE = 128
EPS = 1e-5
MASKED = -float(2 ** 32)
INV_SQRT_D = 1.0 / 16.0
INV_SQRT_DK = 0.25
NORM_MAX = 1e12

LAG = {"self": 0, "proj": 1, "score": 2, "late": 3, "ffn": 4}
LAST_LAG = 4
STEPS = B + LAST_LAG
FULL_FROM, FULL_TO = LAST_LAG, B

QROWS = 96
MROWS = 98
VW = 2 * DK
NPROBS = 4
LOWEST = -3.0e38
PARTS = ((0, 1), (1, 2), (2, 6), (6, 16))
SETUP = 12
BUFFERS_SET = 13
CENTROIDS_MADE = 10

WORK = [
    (0, "max3", "late"), (0, "ctxT", "proj"), (1, "keys", "proj"),
    (2, "x3T", "ffn"), (3, "xT", "self"), (3, "x2T", "proj"),
    (4, "max0", "score"), (4, "logits", "ffn"), (4, "selfY", "self"), (5, "selfV", "self"),
    (5, "queries", "proj"), (5, "logitsT", "ffn"), (6, "selfS", "self"),
    (8, "max1", "score"), (8, "gatesT", "ffn"), (9, "selfPT", "self"),
    (9, "hidden0", "ffn"), (9, "hidden1", "ffn"), (9, "hidden2", "ffn"), (9, "hidden3", "ffn"),
    (10, "values", "proj"), (10, "gate0", "ffn"), (10, "natural0", "late"), (10, "natural1", "late"),
    (11, "selfO", "self"), (11, "gate1", "ffn"), (12, "max2", "score"), (12, "gate2", "ffn"),
    (12, "attT", "late"), (13, "gate3", "ffn"), (14, "wo", "late"), (15, "out", "ffn"),
]
NBANKS = 3
BANK = {name: i % NBANKS for i, (_, name, _) in enumerate(WORK)}
STAGE = {name: stage for _, name, stage in WORK}


def active(s):
    return [g for g in LAG if 0 <= s - LAG[g] < B]


def uses_before(s, name):
    k = BANK[name]
    n = 0
    for step in range(s + 1):
        for _, other, stage in WORK:
            if BANK[other] == k and stage in active(step):
                n += 1
            if step == s and other == name:
                return n


class Step:

    def __init__(self, s, round=None):
        self.s, self.round = s, round
        self.stages = active(s)

    def has(self, stage):
        return stage in self.stages

    def batch(self, stage):
        b = self.s - LAG[stage]
        return b if self.round is None else self.round * 2 + b

    def parity(self, stage):
        return (self.s - LAG[stage]) % 2

    def number(self, per_step, done):
        n = per_step * self.s + done
        return n if self.round is None else self.round * (2 * per_step) + n

    def count(self, stage, per_batch, done):
        n = per_batch * (self.s - LAG[stage]) + done
        return n if self.round is None else self.round * (2 * per_batch) + n

    def half(self, stage, per_batch, done):
        n = per_batch * ((self.s - LAG[stage]) // 2) + done
        return n if self.round is None else self.round * per_batch + n

    def half_before(self, stage, per_batch):
        n = per_batch * ((self.s - LAG[stage] - 1) // 2 + 1)
        return n if self.round is None else self.round * per_batch + n

    def turn(self, name, steps_ago=0):
        s = self.s - steps_ago
        n = uses_before(s, name)
        if self.round is None:
            return n
        return self.round * (uses_before(s + 2, name) - n) + n


def wait(engine, semaphore, value):
    if isinstance(value, int) and value <= 0:
        return
    engine.wait_ge(semaphore, value)


def decoder_layer(nc, x, ctx, mask, Wq, Wk, Wv, wq, wk, wv, wo, w1, b1, w2, b2, cent, route,
                  c_ident, c_onehot, c_cos, c_sin, out):
    with ExitStack() as stack:
        def sb(name, shape, dt=F32):
            return stack.enter_context(nc.sbuf_tensor(name, shape, dt))

        def bank(name):
            return stack.enter_context(nc.psum_tensor(name, [P, 2, 256], F32))

        def sem(name):
            return stack.enter_context(nc.semaphore(name))

        scores_ps = [bank("scores0_ps"), bank("scores1_ps")]
        scoresT_ps = [bank("scoresT0_ps"), bank("scoresT1_ps")]
        pv_ps = bank("pv_ps")
        work_ps = [bank(f"work{k}_ps") for k in range(NBANKS)]

        ident = sb("ident", [P, P])
        ident_b = sb("ident_b", [P, P], BF16)
        cos_k = sb("cos_k", [P, S])
        sin_k = sb("sin_k", [P, S])
        cos_q = sb("cos_q", [P, S])
        sin_q = sb("sin_q", [P, S])
        onehot = sb("onehot", [QROWS, E, P], F32R)
        raw_b = sb("raw_b", [E, DE])
        raw_r = sb("raw_r", [32 + E, D])
        wqk = sb("wqk", [P, C, D])
        wT = sb("wT", [P, 5, C, D])
        w1s = sb("w1s", [P, C, E, DE])
        w2s = sb("w2s", [P, E, D])
        b1T = sb("b1T", [P, E])
        b2s = sb("b2s", [QROWS, D], F32R)
        cwT = sb("cwT", [P, C, 2 * E])
        cst = sb("cst", [E, 8])
        maskN = sb("maskN", [P, T, S])
        maskT = sb("maskT", [P, T, S], BF16)
        alive = sb("alive", [P, T])
        dead = sb("dead", [P, T])
        zero_col = sb("zero_col", [P, 1])
        carrier = sb("carrier", [P, 4])
        half_c = sb("half_c", [P, 8])
        three_c = sb("three_c", [P, 8])
        sixteenth_c = sb("sixteenth_c", [P, T])
        power_c = sb("power_c", [P, 8])

        xr = sb("xr", [P, B, T, D])
        ctx_in = sb("ctx_in", [P, T, D])

        stats = sb("stats", [P, 6, 6])
        mv = sb("mv", [P, 8, 2])
        rs0 = sb("rs0", [P, 8])
        nw = sb("nw", [P, 4, 8])
        rstd = sb("rstd", [P, 8])
        cosn = sb("cosn", [P, 4, T])
        xT = sb("xT", [P, C, S])
        selfY = sb("selfY", [P, C, S])
        selfV = sb("selfV", [P, T, D])
        self_max = sb("self_max", [P, T])
        self_bias = sb("self_bias", [P, T])
        self_sum = sb("self_sum", [P, T])
        self_rec = sb("self_rec", [P, T])
        self_p = sb("self_p", [P, T, S])
        xn = [sb("xn_self", [P, T, D]), sb("xn_proj", [P, T, D]), self_p]
        self_pT = selfY
        ctxT = sb("ctxT", [P, C, S])
        x2T = sb("x2T", [P, C, S])
        rope_a = sb("rope_a", [P, C, S])
        rope_b = sb("rope_b", [P, C, S])
        rope_hi = [sb("rope_hi_k", [P, C, S], F32R), sb("rope_hi_q", [P, C, S], F32R)]
        rope_lo = [sb("rope_lo_k", [P, C, S], F32R), sb("rope_lo_q", [P, C, S], F32R)]
        kstack = [sb("kstack0", [P, H, S], F32R), sb("kstack1", [P, H, S], F32R)]
        qstack = [sb("qstack0", [P, H, S], F32R), sb("qstack1", [P, H, S], F32R)]
        vals = [sb("vals0", [P, T, H, VW]), sb("vals1", [P, T, H, VW])]
        maxima = sb("maxima", [P, T, H])
        mrow_hi = sb("mrow_hi", [4, 2, S], F32R)
        mrow_lo = sb("mrow_lo", [4, 2, S], F32R)
        probs = sb("probs", [P, 4, T, S])
        att = sb("att", [P, 4, S])
        att_rec = sb("att_rec", [P, T, H])
        att_n = self_p
        attT = x2T
        x3T = sb("x3T", [P, C, S])
        logits_s = sb("logits_s", [P, S])
        logits2 = sb("logits2", [P, T, 2 * E])
        logit = sb("logit", [P, T, E])
        top = sb("top", [P, T, 8])
        shifted = sb("shifted", [P, T, E])
        expd = sb("expd", [P, T, E])
        kept = sb("kept", [P, T, E])
        ksum = sb("ksum", [P, T])
        krec = sb("krec", [P, T])
        gates = sb("gates", [P, T, QROWS])
        gatesT = sb("gatesT", [QROWS, S], F32R)
        hidden = sb("hidden", [P, E, S])
        gated = hidden
        raw = [hidden[:, 2 * i:2 * i + 2] for i in range(4)] + [probs[:, i] for i in range(3)]
        raw_mask = probs[:, 3].bitcast(I32)
        onehot_f = att[0:QROWS]
        raw_b2 = selfV[0:QROWS, 0]
        csq = selfV[0:E, 1]
        alive_b = self_p[:, 0].rearrange("p (t m) -> p t m", t=T)

        consts_loaded = sem("consts_loaded")
        weights_loaded = sem("weights_loaded")
        experts_loaded = sem("experts_loaded")
        small_loaded = sem("small_loaded")
        b2_loaded = sem("b2_loaded")
        x_loaded = [sem(f"x_loaded{i}") for i in range(len(PARTS))]
        ctx_loaded = sem("ctx_loaded")
        b2_zeroed = sem("b2_zeroed")
        buffers_set = sem("buffers_set")
        constants_made = sem("constants_made")
        cent_square = sem("cent_square")
        cent_newton = sem("cent_newton")
        setup_formed = sem("setup_formed")
        setup_copied = sem("setup_copied")
        work_ready = [sem(f"work{k}_ready") for k in range(NBANKS)]
        work_copied = [sem(f"work{k}_copied") for k in range(NBANKS)]
        ln_stats = sem("ln_stats")
        ln_moments = sem("ln_moments")
        ln_var = sem("ln_var")
        ln_power = sem("ln_power")
        ln_newton = sem("ln_newton")
        xn_ready = [sem("xn_ready_self"), sem("xn_ready_proj"), sem("xn_ready_ffn")]
        cosn_ready = sem("cosn_ready")
        self_max_found = sem("self_max_found")
        self_bias_ready = sem("self_bias_ready")
        self_rec_ready = sem("self_rec_ready")
        rope_mixed = [sem("rope_mixed_k"), sem("rope_mixed_q")]
        rope_summed = [sem("rope_summed_k"), sem("rope_summed_q")]
        rope_rounded = [sem("rope_rounded_k"), sem("rope_rounded_q")]
        rope_split = [sem("rope_split_k"), sem("rope_split_q")]
        k_stacked = [sem("k_stacked0"), sem("k_stacked1")]
        q_stacked = [sem("q_stacked0"), sem("q_stacked1")]
        scores_ready = sem("scores_ready")
        max_found = sem("max_found")
        mrow_rounded = sem("mrow_rounded")
        mrow_loaded = [sem(f"mrow_loaded{g}") for g in range(4)]
        scoresT_ready = sem("scoresT_ready")
        probs_ready = sem("probs_ready")
        pv_done = sem("pv_done")
        att_copied = sem("att_copied")
        att_rec_ready = sem("att_rec_ready")
        gate_logit = sem("gate_logit")
        gate_top = sem("gate_top")
        gate_shift = sem("gate_shift")
        gate_exp = sem("gate_exp")
        gate_kept = sem("gate_kept")
        gate_rec = sem("gate_rec")
        gates_ready = sem("gates_ready")
        gatesT_rounded = sem("gatesT_rounded")
        stored = sem("stored")

        def W(name):
            return work_ps[BANK[name]]

        def begin(pe, st, name):
            wait(pe, work_copied[BANK[name]], st.turn(name) - 1)

        def ready(engine, st, name):
            engine.wait_ge(work_ready[BANK[name]], st.turn(name))

        def copied(engine, st, name, steps_ago=0):
            engine.wait_ge(work_copied[BANK[name]], st.turn(name, steps_ago))

        def rows(t, b):
            return t[:, b] if isinstance(b, int) else t[:, bass.ds(b, 1)].squeeze(1)

        def run(engine, step):
            for s in range(FULL_FROM):
                step(Step(s))
            with engine.Fori(0, (FULL_TO - FULL_FROM) // 2) as r:
                for u in range(2):
                    step(Step(FULL_FROM + u, r))
            for s in range(FULL_TO, STEPS):
                step(Step(s))

        block = stack.enter_context(nc.Block())

        @block.sync
        def _(sp):
            for dst, src in ((ident[:], c_ident), (cos_k[:], c_cos), (sin_k[:], c_sin), (onehot_f.rearrange("p a b -> p (a b)"), c_onehot)):
                sp.dma_start(dst, src).then_inc(consts_loaded, 16)
            xv = x.rearrange("b (t p) d -> p b t d", p=P)
            cv = ctx.rearrange("b (t p) d -> p b t d", p=P)

            def load(i):
                lo, hi = PARTS[i]
                sp.dma_start(xr[:, lo:hi], xv[:, lo:hi]).then_inc(x_loaded[i], 16)

            load(0)
            for i, w in enumerate((Wq, Wk, Wv, wq, wk, wv, wo)):
                sp.dma_start(raw[i], w.rearrange("(c p) d -> p c d", p=P)).then_inc(weights_loaded, 16)
            sp.dma_start(raw_mask, mask.rearrange("a b (t p) k -> p (a b t) k", p=P)).then_inc(small_loaded, 16)
            sp.dma_start(raw_r[0:E], cent).then_inc(small_loaded, 16)
            sp.dma_start(raw_r[32:32 + E], route).then_inc(small_loaded, 16)
            sp.dma_start(raw_b[:], b1).then_inc(small_loaded, 16)
            sp.wait_ge(b2_zeroed, 1)
            for i in range(3):
                sp.dma_start(raw_b2[32 * i:32 * i + E], b2).then_inc(b2_loaded, 16)
            for i in range(1, len(PARTS)):
                load(i)
            for c in range(C):
                sp.dma_start(w1s[:, c], w1[:, c * P:(c + 1) * P, :].rearrange("e p j -> p e j")).then_inc(experts_loaded, 16)
            sp.dma_start(w2s[:], w2.rearrange("e j d -> j e d")).then_inc(experts_loaded, 16)
            outv = out.rearrange("b (t p) d -> p b t d", p=P)
            sp.wait_ge(buffers_set, BUFFERS_SET)

            def load_context(st):
                if st.has("proj"):
                    copied(sp, st, "ctxT")
                sp.dma_start(ctx_in[:], rows(cv, st.batch("self"))).then_inc(ctx_loaded, 16)

            def send_maxima(st, stage, g):
                par = st.parity(stage)
                copied(sp, st, f"max{g}")
                for row, src in ((QROWS, mrow_hi), (QROWS + 1, mrow_lo)):
                    sp.dma_start(qstack[par][row:row + 1, 4 * g:4 * g + 4, :].bitcast(F32),
                                 src[:, g % 2, :].bitcast(F32)).then_inc(mrow_loaded[g], 16)

            def send_stack(st, j):
                par = st.parity("proj")
                dst = (kstack, qstack)[j][par]
                sent = (k_stacked, q_stacked)[j][par]
                wait(sp, scoresT_ready, st.count("proj", H, -H))
                sp.wait_ge(rope_split[j], st.count("proj", 1, 1))
                for r in range(3):
                    src = rope_lo[j] if r == 1 + j else rope_hi[j]
                    for hh in range(HC):
                        sp.dma_start(dst[DK * r:DK * r + DK, hh:H:HC, :].bitcast(F32),
                                     src[DK * hh:DK * hh + DK].bitcast(F32)).then_inc(sent, 16)

            def step(st):
                if st.has("self"):
                    load_context(st)
                if st.has("late"):
                    send_maxima(st, "late", 3)
                if st.has("score"):
                    send_maxima(st, "score", 0)
                if st.has("proj"):
                    send_stack(st, 0)
                if st.has("score"):
                    send_maxima(st, "score", 1)
                if st.has("proj"):
                    send_stack(st, 1)
                if st.has("score"):
                    send_maxima(st, "score", 2)
                if st.has("ffn"):
                    copied(sp, st, "out")
                    b = st.batch("ffn")
                    sp.dma_start(rows(outv, b), rows(xr, b)).then_inc(stored, 16)

            run(sp, step)
            sp.wait_ge(stored, 16 * B)

        @block.gpsimd
        def _(pool):
            g = nc.gpsimd
            g.memset(raw_b2, 0.0).then_inc(b2_zeroed, 1)
            for i in range(2):
                g.memset(vals[i][:], 1.0).then_inc(buffers_set, 1)
            g.memset(gates[:], 0.0).then_inc(buffers_set, 1)
            g.memset(mv[:], 1.0).then_inc(buffers_set, 1)
            g.memset(logits_s[:], 0.0).then_inc(buffers_set, 1)
            for t, value in ((half_c, 0.5), (three_c, 3.0), (sixteenth_c, 1.0 / 16.0), (power_c, -0.5)):
                g.memset(t[:], value).then_inc(buffers_set, 1)
            pool.wait_ge(buffers_set, BUFFERS_SET)

            pool.wait_ge(cent_square, 2)
            g.tensor_tensor(cst[:, 2:3], cst[:, 0:1], power_c[0:E, 0:1], ALU.pow).then_inc(cent_newton, 1)
            pool.wait_ge(cent_newton, 1)
            g.tensor_tensor(cst[:, 3:4], cst[:, 2:3], cst[:, 2:3], ALU.mult).then_inc(cent_newton, 1)
            pool.wait_ge(cent_newton, 2)
            g.tensor_tensor(cst[:, 4:5], cst[:, 3:4], cst[:, 0:1], ALU.mult).then_inc(cent_newton, 1)
            pool.wait_ge(cent_newton, 3)
            g.tensor_scalar(cst[:, 5:6], cst[:, 4:5], -0.5, 1.5, ALU.mult, ALU.add).then_inc(cent_newton, 1)
            pool.wait_ge(cent_newton, 4)
            g.tensor_tensor(cst[:, 6:7], cst[:, 5:6], cst[:, 2:3], ALU.mult).then_inc(cent_newton, 1)

            def newton(st):
                pool.wait_ge(ln_var, st.number(2, 2))
                g.tensor_tensor(rs0[:], mv[:, :, 1], power_c[:], ALU.pow).then_inc(ln_power, 1)
                pool.wait_ge(ln_power, st.number(1, 1))
                g.tensor_tensor(nw[:, 0], rs0[:], rs0[:], ALU.mult)
                g.tensor_tensor(nw[:, 3], rs0[:], half_c[:], ALU.mult).then_inc(ln_newton, 1)
                pool.wait_ge(ln_newton, st.number(4, 1))
                g.tensor_tensor(nw[:, 1], nw[:, 0], mv[:, :, 1], ALU.mult).then_inc(ln_newton, 1)
                pool.wait_ge(ln_newton, st.number(4, 2))
                g.tensor_tensor(nw[:, 2], three_c[:], nw[:, 1], ALU.subtract).then_inc(ln_newton, 1)
                pool.wait_ge(ln_newton, st.number(4, 3))
                g.tensor_tensor(rstd[:], nw[:, 2], nw[:, 3], ALU.mult).then_inc(ln_newton, 1)

            def inverse_norm(st):
                pool.wait_ge(ln_newton, st.number(4, 4))
                g.tensor_tensor(cosn[:, 0], rstd[:, 6:8], rstd[:, 4:6], ALU.mult).then_inc(cosn_ready, 1)
                pool.wait_ge(cosn_ready, st.count("ffn", 3, 1))
                g.tensor_tensor(cosn[:, 1], cosn[:, 0], mv[:, 4:6, 1], ALU.mult).then_inc(cosn_ready, 1)
                pool.wait_ge(cosn_ready, st.count("ffn", 3, 2))
                g.tensor_tensor(cosn[:, 2], cosn[:, 1], sixteenth_c[:], ALU.mult).then_inc(cosn_ready, 1)

            def rope(st, j):
                sin = (sin_k, sin_q)[j]
                copied(pool, st, ("keys", "queries")[j])
                g.tensor_tensor(rope_b[:], rope_b[:], sin[:].unsqueeze(1).to_broadcast([P, C, S]),
                                ALU.mult).then_inc(rope_mixed[j], 1)
                pool.wait_ge(rope_mixed[j], st.count("proj", 1, 1))
                g.tensor_tensor(rope_a[:], rope_a[:], rope_b[:], ALU.add).then_inc(rope_summed[j], 1)
                pool.wait_ge(rope_rounded[j], st.count("proj", 1, 1))
                g.tensor_tensor(rope_lo[j][:], rope_a[:], rope_hi[j][:].bitcast(F32),
                                ALU.subtract).then_inc(rope_split[j], 1)

            def step(st):
                newton(st)
                if st.has("ffn"):
                    inverse_norm(st)
                if st.has("proj"):
                    rope(st, 0)
                    rope(st, 1)

            run(pool, step)

        @block.scalar
        def _(act):
            a = nc.scalar
            a.preload_act_table(ACT.Exp)
            act.wait_ge(buffers_set, BUFFERS_SET)
            act.wait_ge(setup_copied, SETUP)

            def copy_out(st, name, dst, src=None):
                ready(act, st, name)
                a.copy(dst, W(name)[:] if src is None else src).then_inc(work_copied[BANK[name]], 1)

            def softmax(st, stage, h):
                act.wait_ge(scoresT_ready, st.count(stage, H, h + 1))
                wait(act, pv_done, st.count(stage, H, h + 1 - NPROBS))
                a.activation(probs[:, h % NPROBS], scoresT_ps[h % 2][:], ACT.Exp, bias=zero_col[:],
                             scale=INV_SQRT_DK).then_inc(probs_ready, 1)

            def copy_attention(st, half):
                act.wait_ge(pv_done, st.count("late", H, 8 * half + 8))
                a.copy(att[:, 2 * half:2 * half + 2, :], pv_ps[:]).then_inc(att_copied, 1)

            def rope_round(st, j):
                act.wait_ge(rope_summed[j], st.count("proj", 1, 1))
                wait(act, (k_stacked, q_stacked)[j][1 - st.parity("proj")], st.half_before("proj", 16 * 3 * HC))
                a.copy(rope_hi[j][:], rope_a[:]).then_inc(rope_rounded[j], 1)

            def experts(st):
                for i in range(E // 2):
                    name = f"hidden{i}"
                    ready(act, st, name)
                    for k in range(2):
                        e = 2 * i + k
                        last = a.activation(hidden[:, e], W(name)[:, k], ACT.Gelu, bias=b1T[:, e:e + 1])
                    last.then_inc(work_copied[BANK[name]], 1)
                a.preload_act_table(ACT.Exp)

            def self_softmax(st):
                act.wait_ge(self_bias_ready, st.count("self", 1, 1))
                for t in range(T):
                    last = a.activation(self_p[:, t], W("selfS")[:, t], ACT.Exp, bias=self_bias[:, t:t + 1],
                                        scale=INV_SQRT_D, accum_out=self_sum[:, t:t + 1])
                last.then_inc(work_copied[BANK["selfS"]], 1)

            def step(st):
                for h in range(H):
                    if h < 8 and st.has("late"):
                        softmax(st, "late", h + 8)
                    if h >= 8 and st.has("score"):
                        softmax(st, "score", h - 8)
                    if h == 0 and st.has("late"):
                        copy_attention(st, 0)
                    if h == 9 and st.has("late"):
                        copy_attention(st, 1)
                    if h == 0 and st.has("proj"):
                        copy_out(st, "ctxT", ctxT[:])
                    if h == 2 and st.has("ffn"):
                        copy_out(st, "x3T", x3T[:])
                    if h == 3 and st.has("self"):
                        copy_out(st, "xT", xT[:])
                    if h == 3 and st.has("proj"):
                        copy_out(st, "x2T", x2T[:])
                    if h == 4 and st.has("ffn"):
                        copy_out(st, "logits", logits_s[0:2 * E, :], W("logits")[0:2 * E, 0, :])
                    if h == 4 and st.has("proj"):
                        rope_round(st, 0)
                    if h == 5 and st.has("self"):
                        copy_out(st, "selfV", selfV[:])
                    if h == 6 and st.has("ffn"):
                        act.wait_ge(gate_shift, st.count("ffn", 1, 1))
                        a.activation(expd[:], shifted[:], ACT.Exp, bias=zero_col[:]).then_inc(gate_exp, 1)
                    if h == 7 and st.has("self"):
                        self_softmax(st)
                    if h == 8 and st.has("ffn"):
                        ready(act, st, "gatesT")
                        a.copy(gatesT[:], W("gatesT")[0:QROWS, 0, :]).then_inc(gatesT_rounded, 1)
                    if h == 8 and st.has("proj"):
                        rope_round(st, 1)
                    if h == 9 and st.has("self"):
                        copy_out(st, "selfPT", self_pT[:])
                    if h == 9 and st.has("ffn"):
                        experts(st)
                    if h == 10 and st.has("proj"):
                        copy_out(st, "values", vals[st.parity("proj")][:, :, :, 0:DK],
                                 W("values")[:].rearrange("p t (h d) -> p t h d", h=H))

            run(act, step)

        @block.vector
        def _(dve):
            v = nc.vector
            made = [0]

            def chain(ins):
                made[0] += 1
                ins.then_inc(constants_made, 1)
                dve.wait_ge(constants_made, made[0])

            chain(v.memset(zero_col[:], 0.0))
            for i in range(2):
                v.memset(qstack[i][:].bitcast(F32), 0.0).then_inc(buffers_set, 1)
                chain(v.memset(kstack[i][:].bitcast(F32), 0.0))
                v.memset(kstack[i][QROWS:MROWS].bitcast(F32), -1.0).then_inc(buffers_set, 1)
            dve.wait_ge(consts_loaded, 64)
            v.tensor_copy(ident_b[:], ident[:]).then_inc(setup_copied, 1)
            v.tensor_copy(onehot[:], onehot_f.rearrange("p a b -> p (a b)").rearrange("p (e j) -> p e j", e=E)).then_inc(setup_copied, 1)
            dve.wait_ge(small_loaded, 64)
            v.tensor_tensor_reduce(csq, raw_r[0:E], raw_r[0:E], 1.0, 0.0, ALU.mult, ALU.add,
                                   cst[:, 7:8]).then_inc(cent_square, 1)
            dve.wait_ge(cent_square, 1)
            v.tensor_scalar(cst[:, 0:1], cst[:, 7:8], 1e-24, None, ALU.max).then_inc(cent_square, 1)
            chain(v.tensor_scalar(maskN[:], raw_mask, 0.0, None, ALU.not_equal))
            chain(v.tensor_reduce(alive[:], maskN[:], AX_X, ALU.max))
            chain(v.tensor_scalar(dead[:], alive[:], -1.0, 1.0, ALU.mult, ALU.add))
            for t in range(T):
                v.tensor_scalar(alive_b[:, t], ident[:], 0.0, alive[:, t:t + 1], ALU.mult, ALU.add)
                chain(v.tensor_scalar(maskN[:, t], maskN[:, t], dead[:, t:t + 1], 1.0, ALU.max, ALU.subtract))
            chain(v.tensor_scalar(maskN[:], maskN[:], -MASKED, None, ALU.mult))
            dve.wait_ge(cent_newton, 5)
            chain(v.tensor_scalar(raw_r[0:E], raw_r[0:E], cst[:, 6:7], None, ALU.mult))
            for i in range(SETUP - 2):
                dve.wait_ge(setup_formed, i + 1)
                src = scores_ps[i % 2]
                if i == 0:
                    ins = v.tensor_copy(wqk[:], src[:])
                elif i <= 5:
                    ins = v.tensor_copy(wT[:, i - 1], src[:])
                elif i == 6:
                    v.tensor_copy(cwT[:, :, 0:E], src[:, :, 0:E])
                    ins = v.tensor_copy(cwT[:, :, E:2 * E], src[:, :, 32:32 + E])
                elif i == 7:
                    ins = v.tensor_copy(b1T[:], src[:, 0, 0:E])
                elif i == 8:
                    v.tensor_tensor(cos_q[:], cos_k[:], src[:, 0, :], ALU.mult)
                    ins = v.tensor_tensor(sin_q[:], sin_k[:], src[:, 0, :], ALU.mult)
                else:
                    ins = v.tensor_copy(maskT[:], src[:])
                ins.then_inc(setup_copied, 1)
            dve.wait_ge(b2_loaded, 48)
            chain(v.tensor_copy(b2s[:], raw_b2))
            chain(v.tensor_tensor(b2s[64:QROWS], raw_b2[64:QROWS], b2s[64:QROWS].bitcast(F32), ALU.subtract))
            dve.wait_ge(buffers_set, BUFFERS_SET)

            def carry(i):
                v.memset(carrier[:, i:i + 1], 0.0)

            def layer_norm_stats(st):
                if st.has("self"):
                    for i, (lo, hi) in enumerate(PARTS):
                        if st.round is None and st.s == lo:
                            dve.wait_ge(x_loaded[i], 16)
                if st.s == FULL_FROM:
                    for i, (lo, hi) in enumerate(PARTS):
                        if lo >= FULL_FROM:
                            dve.wait_ge(x_loaded[i], 16)
                done = [i for i, g in enumerate(("self", "proj", "ffn")) if st.has(g)]
                for i in done:
                    x_rows = rows(xr, st.batch(("self", "proj", "ffn")[i]))
                    for t in range(T):
                        last = v.bn_stats(stats[:, 2 * i + t], x_rows[:, t])
                last.then_inc(ln_stats, 1)
                dve.wait_ge(ln_stats, st.number(1, 1))
                carry(2)
                for i in done:
                    for t in range(T):
                        last = v.bn_aggr(mv[:, 2 * i + t], stats[:, 2 * i + t])
                last.then_inc(ln_moments, 1)
                dve.wait_ge(ln_moments, st.number(1, 1))
                v.tensor_scalar(mv[:, 6:8, 1], mv[:, 4:6, 1], 1e-37, None, ALU.max).then_inc(ln_var, 1)
                dve.wait_ge(ln_var, st.number(2, 1))
                v.tensor_scalar(mv[:, 0:6, 1], mv[:, 0:6, 1], EPS, None, ALU.add).then_inc(ln_var, 1)

            def normalise(st, stage, i):
                dve.wait_ge(ln_newton, st.number(4, 4))
                x_rows = rows(xr, st.batch(stage))
                for t in range(T):
                    k = 2 * i + t
                    last = v.tensor_scalar(xn[i][:, t], x_rows[:, t], mv[:, k, 0:1], rstd[:, k:k + 1],
                                           ALU.subtract, ALU.mult)
                last.then_inc(xn_ready[i], 1)

            def copy_out(st, name, dst):
                ready(dve, st, name)
                v.tensor_copy(dst, W(name)[:]).then_inc(work_copied[BANK[name]], 1)

            def head_max(st, h):
                dve.wait_ge(scores_ready, st.count("score", H, h + 1))
                carry(h % 2)
                for t in range(T):
                    s_ps = scores_ps[h % 2][:, t]
                    last = v.tensor_tensor_reduce(s_ps, s_ps, maskN[:, t], 1.0, LOWEST, ALU.add, ALU.max,
                                                  maxima[:, t, h:h + 1])
                last.then_inc(max_found, 1)

            def round_maxima(st, stage, g):
                name = f"max{g}"
                ready(dve, st, name)
                wait(dve, mrow_loaded[(g + 2) % 4], st.count(stage, 32, 32 if g >= 2 else 0))
                v.tensor_copy(mrow_hi[:, g % 2], W(name)[0:4, 0, :]).then_inc(mrow_rounded, 1)
                dve.wait_ge(mrow_rounded, st.count(stage, 4, g + 1))
                v.tensor_tensor(mrow_lo[:, g % 2], W(name)[0:4, 0, :], mrow_hi[:, g % 2].bitcast(F32),
                                ALU.subtract).then_inc(work_copied[BANK[name]], 1)

            def turn_pairs(st, j):
                name = ("keys", "queries")[j]
                ready(dve, st, name)
                cos = (cos_k, cos_q)[j]
                wait(dve, rope_split[1 - j], st.count("proj", 1, j))
                v.tensor_tensor(rope_a[:], W(name)[:], cos[:].unsqueeze(1).to_broadcast([P, C, S]), ALU.mult)
                v.stream_shuffle(rope_b[:], W(name)[:], [i ^ 1 for i in range(32)]).then_inc(
                    work_copied[BANK[name]], 1)

            def self_maximum(st):
                ready(dve, st, "selfS")
                v.tensor_reduce(self_max[:], W("selfS")[:], AX_X, ALU.max).then_inc(self_max_found, 1)
                dve.wait_ge(self_max_found, st.count("self", 1, 1))
                v.tensor_scalar(self_bias[:], self_max[:], -INV_SQRT_D, None, ALU.mult).then_inc(self_bias_ready, 1)

            def add_self_attention(st):
                copied(dve, st, "selfS")
                v.reciprocal(self_rec[:], self_sum[:]).then_inc(self_rec_ready, 1)
                dve.wait_ge(self_rec_ready, st.count("self", 1, 1))
                ready(dve, st, "selfO")
                x_rows = rows(xr, st.batch("self"))
                for t in range(T):
                    last = v.scalar_tensor_tensor(x_rows[:, t], W("selfO")[:, t], self_rec[:, t:t + 1], x_rows[:, t],
                                                  ALU.mult, ALU.add)
                last.then_inc(work_copied[BANK["selfO"]], 1)

            def add_to_stream(st, name, stage):
                ready(dve, st, name)
                x_rows = rows(xr, st.batch(stage))
                v.tensor_tensor(x_rows, x_rows, W(name)[:], ALU.add).then_inc(work_copied[BANK[name]], 1)

            def normalise_attention(st, t):
                name = f"natural{t}"
                ready(dve, st, name)
                heads = W(name)[:].rearrange("p a (g w) -> p (a g) w", w=VW)
                v.reciprocal(att_rec[:, t], heads[:, :, DK]).then_inc(att_rec_ready, 1)
                dve.wait_ge(att_rec_ready, st.count("late", T, t + 1))
                v.tensor_tensor(att_n[:, t].rearrange("p (h d) -> p h d", h=H), heads[:, :, 0:DK], att_rec[:, t].unsqueeze(2).to_broadcast([P, H, DK]),
                                ALU.mult).then_inc(work_copied[BANK[name]], 1)

            def gate_logits(st):
                dve.wait_ge(cosn_ready, st.count("ffn", 3, 3))
                ready(dve, st, "logitsT")
                v.tensor_scalar(cosn[:, 3], cosn[:, 2], NORM_MAX, None, ALU.min)
                v.tensor_copy(logits2[:], W("logitsT")[:, 0].rearrange("p (t e) -> p t e", t=T)[:, :, 0:2 * E]).then_inc(
                    work_copied[BANK["logitsT"]], 1)
                copied(dve, st, "logitsT")
                for t in range(T):
                    last = v.scalar_tensor_tensor(logit[:, t], logits2[:, t, 0:E], cosn[:, 3, t:t + 1],
                                                  logits2[:, t, E:2 * E], ALU.mult, ALU.add)
                last.then_inc(gate_logit, 1)
                dve.wait_ge(gate_logit, st.count("ffn", 1, 1))
                carry(3)
                for t in range(T):
                    last = v.max(top[:, t], logit[:, t])
                last.then_inc(gate_top, 1)
                dve.wait_ge(gate_top, st.count("ffn", 1, 1))
                for t in range(T):
                    last = v.tensor_scalar(shifted[:, t], logit[:, t], top[:, t, 0:1], None, ALU.subtract)
                last.then_inc(gate_shift, 1)

            def gate_weights(st):
                dve.wait_ge(gate_exp, st.count("ffn", 1, 1))
                for t in range(T):
                    last = v.scalar_tensor_tensor(kept[:, t], logit[:, t], top[:, t, 1:2], expd[:, t],
                                                  ALU.is_ge, ALU.mult, accum_out=ksum[:, t:t + 1])
                last.then_inc(gate_kept, 1)
                dve.wait_ge(gate_kept, st.count("ffn", 1, 1))
                v.reciprocal(krec[:], ksum[:]).then_inc(gate_rec, 1)
                dve.wait_ge(gate_rec, st.count("ffn", 1, 1))
                for t in range(T):
                    last = v.tensor_scalar(gates[:, t].rearrange("p (r c) -> p r c", r=3)[:, :, 0:E],
                                           kept[:, t].unsqueeze(1).to_broadcast([P, 3, E]),
                                           krec[:, t:t + 1], None, ALU.mult)
                last.then_inc(gates_ready, 1)

            def gates_low_part(st):
                dve.wait_ge(gatesT_rounded, st.count("ffn", 1, 1))
                v.tensor_tensor(gatesT[32:32 + E], W("gatesT")[32:32 + E, 0, :], gatesT[32:32 + E].bitcast(F32),
                                ALU.subtract).then_inc(work_copied[BANK["gatesT"]], 1)

            def apply_gate(st, i):
                name = f"gate{i}"
                copied(dve, st, f"hidden{i}")
                ready(dve, st, name)
                v.tensor_tensor(gated[:, 2 * i:2 * i + 2], hidden[:, 2 * i:2 * i + 2], W(name)[:], ALU.mult).then_inc(
                    work_copied[BANK[name]], 1)

            def step(st):
                layer_norm_stats(st)
                for h in range(H):
                    if st.has("score"):
                        head_max(st, h)
                    if h == 0 and st.has("late"):
                        round_maxima(st, "late", 3)
                    if h == 1 and st.has("ffn"):
                        normalise(st, "ffn", 2)
                    if h == 1 and st.has("proj"):
                        turn_pairs(st, 0)
                    if h == 2 and st.has("self"):
                        normalise(st, "self", 0)
                    if h == 2 and st.has("proj"):
                        normalise(st, "proj", 1)
                    if h in (4, 8, 12) and st.has("score"):
                        round_maxima(st, "score", h // 4 - 1)
                    if h == 4 and st.has("self"):
                        copy_out(st, "selfY", selfY[:])
                    if h == 5 and st.has("proj"):
                        turn_pairs(st, 1)
                    if h == 5 and st.has("ffn"):
                        gate_logits(st)
                    if h == 6 and st.has("self"):
                        self_maximum(st)
                    if h == 7 and st.has("ffn"):
                        gate_weights(st)
                    if h == 8 and st.has("ffn"):
                        gates_low_part(st)
                    if h == 10 and st.has("ffn"):
                        apply_gate(st, 0)
                    if h == 10 and st.has("late"):
                        normalise_attention(st, 0)
                        normalise_attention(st, 1)
                    if h == 11 and st.has("self"):
                        add_self_attention(st)
                    if h in (11, 12, 13) and st.has("ffn"):
                        apply_gate(st, h - 10)
                    if h == 12 and st.has("self"):
                        copied(dve, st, "selfO")
                    if h == 12 and st.has("late"):
                        copy_out(st, "attT", attT[:])
                    if h == 14 and st.has("late"):
                        add_to_stream(st, "wo", "late")
                    if h == 15 and st.has("ffn"):
                        add_to_stream(st, "out", "ffn")
                    if h == 15 and st.has("late"):
                        copied(dve, st, "wo")

            run(dve, step)

        @block.tensor
        def _(pe):
            t_ = nc.tensor

            def transposed(dst, src, fill=None):
                for c in range(C):
                    for t in range(T):
                        last = t_.transpose(dst[:, c, t * P:(t + 1) * P], src[:, t, c * P:(c + 1) * P], ident[:])
                return last

            def product(dst, left, right):
                for m in range(2):
                    for c in range(C):
                        last = t_.matmul(dst[:, m], left[:, c, m * P:(m + 1) * P], right[:, c, :],
                                         start=c == 0, stop=c == C - 1)
                return last

            pe.wait_ge(consts_loaded, 64)
            pe.wait_ge(weights_loaded, 16 * 7)
            for i in range(SETUP - 2):
                wait(pe, setup_copied, i - 1 + 2)
                dst = scores_ps[i % 2]
                if i == 0:
                    last = product(dst, raw[0], raw[1])
                elif i <= 5:
                    last = transposed(dst, raw[1 + i])
                elif i == 6:
                    pe.wait_ge(small_loaded, 64)
                    pe.wait_ge(constants_made, CENTROIDS_MADE)
                    for c in range(C):
                        last = t_.transpose(dst[:, c, 0:32 + E], raw_r[0:32 + E, c * P:(c + 1) * P],
                                            ident[0:32 + E, 0:32 + E])
                elif i == 7:
                    last = t_.transpose(dst[:, 0, 0:E], raw_b[:], ident[0:E, 0:E])
                elif i == 8:
                    for t in range(T):
                        last = t_.matmul(dst[:, 0, t * P:(t + 1) * P], alive_b[:, t], ident[:], start=True, stop=True)
                else:
                    last = transposed(dst, maskN[:])
                last.then_inc(setup_formed, 1)
            pe.wait_ge(setup_copied, SETUP)
            pe.wait_ge(buffers_set, BUFFERS_SET)

            def finish(last, name):
                last.then_inc(work_ready[BANK[name]], 1)

            def scores(st, h):
                par = st.parity("score")
                if h == 0:
                    pe.wait_ge(k_stacked[par], st.half("score", 16 * 3 * HC, 16 * 3 * HC))
                    pe.wait_ge(q_stacked[par], st.half("score", 16 * 3 * HC, 16 * 3 * HC))
                wait(pe, max_found, st.count("score", H, h - 1))
                for t in range(T):
                    last = t_.matmul(scores_ps[h % 2][:, t], qstack[par][0:QROWS, h, t * P:(t + 1) * P],
                                     kstack[par][0:QROWS, h, :], start=True, stop=True)
                last.then_inc(scores_ready, 1)

            def scoresT(st, stage, h):
                par = st.parity(stage)
                if h % 4 == 0:
                    pe.wait_ge(mrow_loaded[h // 4], st.count(stage, 32, 32))
                wait(pe, probs_ready, st.count(stage, H, h - 1))
                for t in range(T):
                    t_.matmul(scoresT_ps[h % 2][:, t], kstack[par][0:MROWS, h, t * P:(t + 1) * P],
                              qstack[par][0:MROWS, h, :], start=True, stop=False)
                    last = t_.matmul(scoresT_ps[h % 2][:, t], ident_b[:], maskT[:, t], start=False, stop=True)
                last.then_inc(scoresT_ready, 1)

            def values_product(st, stage, h):
                par = st.parity(stage)
                pe.wait_ge(probs_ready, st.count(stage, H, h + 1))
                if h % 8 == 0:
                    wait(pe, att_copied, st.count(stage, 2, h // 8))
                j = h % 4
                for t in range(T):
                    last = t_.matmul(pv_ps[VW * j:VW * j + VW, h // 4 % 2], vals[par][:, t, h, :],
                                     probs[:, h % NPROBS, t], start=t == 0, stop=t == T - 1)
                last.then_inc(pv_done, 1)

            def work(st, name):
                begin(pe, st, name)
                ps = W(name)

                def need(other):
                    if BANK[other] != BANK[name]:
                        copied(pe, st, other)

                if name in ("xT", "x2T", "x3T"):
                    i = ("xT", "x2T", "x3T").index(name)
                    pe.wait_ge(xn_ready[i], st.count(STAGE[name], 1, 1))
                    last = transposed(ps, xn[i])
                elif name == "ctxT":
                    pe.wait_ge(ctx_loaded, st.count("proj", 16, 16))
                    last = transposed(ps, ctx_in)
                elif name == "keys":
                    need("ctxT")
                    last = product(ps, wT[:, 2], ctxT[:])
                elif name == "queries":
                    need("x2T")
                    last = product(ps, wT[:, 1], x2T[:])
                elif name == "values":
                    last = product(ps, ctxT[:], wT[:, 3])
                elif name == "selfY":
                    need("xT")
                    last = product(ps, wqk[:], xT[:])
                elif name == "selfV":
                    last = product(ps, xT[:], wT[:, 0])
                elif name == "selfS":
                    need("selfY")
                    last = product(ps, selfY[:], xT[:])
                elif name == "selfPT":
                    need("selfS")
                    last = transposed(ps, self_p[:])
                elif name == "selfO":
                    need("selfPT")
                    last = product(ps, self_pT[:], selfV[:])
                elif name.startswith("max"):
                    g = int(name[3])
                    stage = STAGE[name]
                    pe.wait_ge(max_found, st.count(stage, H, 4 * g + 4))
                    for t in range(T):
                        last = t_.transpose(ps[0:4, 0, t * P:(t + 1) * P], maxima[:, t, 4 * g:4 * g + 4], ident[:])
                elif name == "logits":
                    need("x3T")
                    for c in range(C):
                        last = t_.matmul(ps[0:2 * E, 0, :], cwT[:, c, :], x3T[:, c, :], start=c == 0, stop=c == C - 1)
                elif name == "logitsT":
                    need("logits")
                    for t in range(T):
                        last = t_.transpose(ps[:, 0, t * P:(t + 1) * P], logits_s[:, t * P:(t + 1) * P], ident[:])
                elif name == "gatesT":
                    pe.wait_ge(gates_ready, st.count("ffn", 1, 1))
                    for t in range(T):
                        last = t_.transpose(ps[0:QROWS, 0, t * P:(t + 1) * P], gates[:, t, :], ident[:])
                elif name.startswith("hidden"):
                    i = int(name[6])
                    if i == 0 and st.round is None and st.s == LAG["ffn"] or st.s == FULL_FROM:
                        pe.wait_ge(experts_loaded, 48)
                    for k in range(2):
                        for c in range(C):
                            last = t_.matmul(ps[:, k], w1s[:, c, 2 * i + k, :], x3T[:, c, :],
                                             start=c == 0, stop=c == C - 1)
                elif name.startswith("gate"):
                    i = int(name[4])
                    if i == 0:
                        need("gatesT")
                    for k in range(2):
                        last = t_.matmul(ps[:, k], onehot[:, 2 * i + k, :], gatesT[:], start=True, stop=True)
                elif name.startswith("natural"):
                    t = int(name[7])
                    pe.wait_ge(att_copied, st.count("late", 2, 2))
                    flat = ps[:].rearrange("p a b -> p (a b)")
                    for g in range(4):
                        last = t_.transpose(flat[:, g * P:(g + 1) * P], att[:, g, t * P:(t + 1) * P], ident[:])
                elif name == "attT":
                    need("natural1")
                    last = transposed(ps, att_n[:])
                elif name == "wo":
                    need("attT")
                    last = product(ps, attT[:], wT[:, 4])
                elif name == "out":
                    need("gate3")
                    for t in range(T):
                        t_.matmul(ps[:, t], gatesT[:, t * P:(t + 1) * P], b2s[:], start=True, stop=False)
                        for e in range(E):
                            last = t_.matmul(ps[:, t], gated[:, e, t * P:(t + 1) * P], w2s[:, e, :],
                                             start=False, stop=e == E - 1)
                finish(last, name)

            def step(st):
                for h in range(H):
                    if h < 8 and st.has("late"):
                        scoresT(st, "late", h + 8)
                    if h >= 8 and st.has("score"):
                        scoresT(st, "score", h - 8)
                    if st.has("score"):
                        scores(st, h)
                    for slot, name, stage in WORK:
                        if slot == h and st.has(stage):
                            work(st, name)
                    if h == 13 and st.has("proj"):
                        copied(pe, st, "values")
                    if h <= 8 and st.has("late"):
                        values_product(st, "late", h + 7)
                    if h >= 9 and st.has("score"):
                        values_product(st, "score", h - 9)

            run(pe, step)


_INS = ["x", "ctx_1024", "mask_1x1xSxS2_ik0", "L0_attn_Wq", "L0_attn_Wk", "L0_attn_Wv", "L0_xattn_wq", "L0_xattn_wk",
        "L0_xattn_wv", "L0_xattn_wo", "L0_ffn_w1", "L0_ffn_b1", "L0_ffn_w2", "L0_ffn_b2", "L0_ffn_centroids",
        "L0_ffn_w_route"]


def shape_constants():
    import numpy as np
    ident = np.eye(P, dtype=np.float32)
    onehot = np.zeros((QROWS, E, P), np.float32)
    for e in range(E):
        onehot[e, e] = 1.0
        onehot[32 + e, e] = 1.0
    inv_freq = (np.float32(1.0) / np.float32(10000.0) ** (np.arange(0, DK, 2, dtype=np.float32) / np.float32(DK)))
    angle = np.arange(S, dtype=np.float32)[None, :] * np.concatenate([inv_freq, inv_freq])[:, None].astype(np.float32)
    sign = np.where(np.arange(DK) % 2 == 0, -1.0, 1.0).astype(np.float32)[:, None]
    cos = np.tile(np.cos(angle).astype(np.float32), (HC, 1))
    sin = np.tile(np.sin(angle).astype(np.float32) * sign, (HC, 1))
    return {"c_ident": ident, "c_onehot": onehot.reshape(QROWS, E * P), "c_cos": cos, "c_sin": sin}


def kernel(**inputs):
    import numpy as np
    import concourse.bacc as bacc
    from concourse import mybir as _mybir
    from concourse.bass_utils import run_bass_kernel_spmd

    nc = bacc.Bacc("TRN2", target_bir_lowering=False, num_devices=1)
    arrays, args = {}, []
    for name in _INS:
        a = np.ascontiguousarray(inputs[name])
        arrays[f"in_{name}"] = a
        args.append(nc.dram_tensor(f"in_{name}", a.shape, _mybir.dt.from_np(a.dtype), kind="ExternalInput").ap())
    for name, a in shape_constants().items():
        arrays[name] = np.ascontiguousarray(a)
        args.append(nc.dram_tensor(name, a.shape, _mybir.dt.from_np(a.dtype), kind="ExternalInput").ap())
    args.append(nc.dram_tensor("out_dram", (B, S, D), F32, kind="ExternalOutput").ap())
    decoder_layer(nc, *args)
    r = run_bass_kernel_spmd(nc, [arrays], core_ids=[0])
    return r.results[0]["out_dram"]
```

```python
from contextlib import ExitStack

import concourse.bass as bass
from concourse import mybir

ALU = mybir.AluOpType
ACT = mybir.ActivationFunctionType
AX_X = mybir.AxisListType.X
F32 = mybir.dt.float32
F32R = mybir.dt.float32r
BF16 = mybir.dt.bfloat16
I32 = mybir.dt.int32

P = 128
B = 16
S = 256
T = S // P
D = 256
C = D // P
H = 16
DK = D // H
HC = P // DK
E = 8
DE = 128
EPS = 1e-5
MASKED = -float(2 ** 32)
INV_SQRT_D = 1.0 / 16.0
INV_SQRT_DK = 0.25
NORM_MAX = 1e12

LAG = {"self": 0, "proj": 1, "score": 2, "late": 3, "ffn": 4}
LAST_LAG = 4
STEPS = B + LAST_LAG
FULL_FROM, FULL_TO = LAST_LAG, B

QROWS = 96
STACKED = 6 * 16
MROWS = 98
VW = 2 * DK
NPROBS = 4
LOWEST = -3.0e38
RING = 8
PARTS = ((0, 1), (1, 2), (2, 4))
SETUP = 11
SMALL_SET = 7
BUFFERS_SET = 4
STACKS_SET = 3
CENTROIDS_MADE = 8

WORK = [
    [0, 'max3', 'late'],
    [0, 'ctxT', 'proj'],
    [0, 'x3T', 'ffn'],
    [1, 'x2T', 'proj'],
    [1, 'keys', 'proj'],
    [2, 'logits', 'ffn'],
    [3, 'logitsT', 'ffn'],
    [3, 'xT', 'self'],
    [3, 'queries', 'proj'],
    [5, 'max0', 'score'],
    [5, 'selfY', 'self'],
    [6, 'selfV', 'self'],
    [6, 'selfS', 'self'],
    [6, 'gatesT', 'ffn'],
    [7, 'hidden0', 'ffn'],
    [7, 'gate0', 'ffn'],
    [7, 'hidden1', 'ffn'],
    [7, 'gate1', 'ffn'],
    [7, 'hidden2', 'ffn'],
    [7, 'gate2', 'ffn'],
    [7, 'hidden3', 'ffn'],
    [7, 'gate3', 'ffn'],
    [8, 'max1', 'score'],
    [8, 'selfPT', 'self'],
    [9, 'values', 'proj'],
    [10, 'natural0', 'late'],
    [10, 'natural1', 'late'],
    [11, 'selfO', 'self'],
    [11, 'attT', 'late'],
    [11, 'max2', 'score'],
    [13, 'wo', 'late'],
    [15, 'out', 'ffn'],
]
HEAD_WORK = [
    [0, 'max3', 'late'],
    [0, 'ctxT', 'proj'],
    [1, 'x2T', 'proj'],
    [2, 'keys', 'proj'],
    [3, 'xT', 'self'],
    [3, 'queries', 'proj'],
    [5, 'max0', 'score'],
    [5, 'selfY', 'self'],
    [6, 'selfV', 'self'],
    [6, 'selfS', 'self'],
    [8, 'max1', 'score'],
    [9, 'selfPT', 'self'],
    [9, 'values', 'proj'],
    [10, 'natural0', 'late'],
    [10, 'natural1', 'late'],
    [12, 'attT', 'late'],
    [12, 'max2', 'score'],
    [12, 'selfO', 'self'],
    [13, 'wo', 'late'],
]
TAIL_WORK = [
    [0, 'max3', 'late'],
    [0, 'x3T', 'ffn'],
    [0, 'ctxT', 'proj'],
    [1, 'x2T', 'proj'],
    [2, 'keys', 'proj'],
    [2, 'logits', 'ffn'],
    [3, 'logitsT', 'ffn'],
    [3, 'queries', 'proj'],
    [5, 'max0', 'score'],
    [7, 'gatesT', 'ffn'],
    [7, 'hidden0', 'ffn'],
    [7, 'gate0', 'ffn'],
    [7, 'hidden1', 'ffn'],
    [7, 'gate1', 'ffn'],
    [7, 'hidden2', 'ffn'],
    [7, 'gate2', 'ffn'],
    [7, 'hidden3', 'ffn'],
    [7, 'gate3', 'ffn'],
    [8, 'max1', 'score'],
    [9, 'values', 'proj'],
    [10, 'natural0', 'late'],
    [10, 'natural1', 'late'],
    [11, 'attT', 'late'],
    [12, 'max2', 'score'],
    [13, 'wo', 'late'],
    [15, 'out', 'ffn'],
]
NBANKS = 3
BANK = {name: i % NBANKS for i, (_, name, _) in enumerate(WORK)}
STAGE = {name: stage for _, name, stage in WORK}


SPLIT = ("ctxT", "x3T", "x2T", "xT", "selfY", "selfV", "selfPT", "attT")

ACT_WORK = [
    [0, 'ctxT', 'proj'],
    [0, 'x3T', 'ffn'],
    [1, 'attention0', 'late'],
    [1, 'x2T', 'proj'],
    [2, 'logits', 'ffn'],
    [2, 'xT', 'self'],
    [2, 'round_k', 'proj'],
    [4, 'selfY', 'self'],
    [4, 'gate_exp', 'ffn'],
    [6, 'round_q', 'proj'],
    [6, 'selfV', 'self'],
    [6, 'softmax', 'self'],
    [6, 'gatesT', 'ffn'],
    [7, 'gelu0', 'ffn'],
    [7, 'gelu1', 'ffn'],
    [7, 'gated0', 'ffn'],
    [7, 'gelu2', 'ffn'],
    [7, 'gated1', 'ffn'],
    [7, 'gelu3', 'ffn'],
    [7, 'gated2', 'ffn'],
    [8, 'attention1', 'late'],
    [8, 'gated3', 'ffn'],
    [8, 'selfPT', 'self'],
    [9, 'values', 'proj'],
    [10, 'attT', 'late'],
]
HEAD_ACT_WORK = [
    [0, 'attention0', 'late'],
    [0, 'ctxT', 'proj'],
    [1, 'x2T', 'proj'],
    [2, 'xT', 'self'],
    [3, 'round_k', 'proj'],
    [4, 'selfY', 'self'],
    [6, 'selfV', 'self'],
    [7, 'softmax', 'self'],
    [7, 'round_q', 'proj'],
    [7, 'attention1', 'late'],
    [9, 'selfPT', 'self'],
    [9, 'values', 'proj'],
    [11, 'attT', 'late'],
]
TAIL_ACT_WORK = [
    [0, 'x3T', 'ffn'],
    [0, 'attention0', 'late'],
    [0, 'ctxT', 'proj'],
    [1, 'x2T', 'proj'],
    [2, 'logits', 'ffn'],
    [3, 'round_k', 'proj'],
    [4, 'gate_exp', 'ffn'],
    [6, 'round_q', 'proj'],
    [6, 'gatesT', 'ffn'],
    [7, 'gelu0', 'ffn'],
    [7, 'gelu1', 'ffn'],
    [7, 'gated0', 'ffn'],
    [7, 'gelu2', 'ffn'],
    [7, 'gated1', 'ffn'],
    [7, 'gated2', 'ffn'],
    [7, 'gelu3', 'ffn'],
    [8, 'attention1', 'late'],
    [8, 'gated3', 'ffn'],
    [9, 'values', 'proj'],
    [10, 'attT', 'late'],
]

DVE_WORK = [
    [0, 'max3', 'late'],
    [0, 'ctxT', 'proj'],
    [0, 'moments_self', 'self'],
    [0, 'x3T', 'ffn'],
    [1, 'turn_k', 'proj'],
    [1, 'x2T', 'proj'],
    [2, 'normal_self', 'self'],
    [2, 'gate_logits', 'ffn'],
    [3, 'xT', 'self'],
    [3, 'turn_q', 'proj'],
    [5, 'max0', 'score'],
    [5, 'selfY', 'self'],
    [5, 'gate_weights', 'ffn'],
    [6, 'selfV', 'self'],
    [6, 'self_max', 'self'],
    [6, 'gates_low', 'ffn'],
    [7, 'gate0', 'ffn'],
    [7, 'gate1', 'ffn'],
    [7, 'low0', 'ffn'],
    [7, 'gate2', 'ffn'],
    [7, 'low1', 'ffn'],
    [7, 'gate3', 'ffn'],
    [7, 'low2', 'ffn'],
    [8, 'max1', 'score'],
    [8, 'low3', 'ffn'],
    [8, 'selfPT', 'self'],
    [10, 'natural0', 'late'],
    [10, 'natural1', 'late'],
    [11, 'add_self', 'self'],
    [11, 'attT', 'late'],
    [11, 'max2', 'score'],
    [13, 'wo', 'late'],
    [13, 'moments_ahead', 'any'],
    [14, 'normal_ahead', 'any'],
    [15, 'out', 'ffn'],
]
HEAD_DVE_WORK = [
    [0, 'max3', 'late'],
    [0, 'moments_self', 'self'],
    [0, 'ctxT', 'proj'],
    [1, 'x2T', 'proj'],
    [2, 'turn_k', 'proj'],
    [2, 'normal_self', 'self'],
    [3, 'xT', 'self'],
    [3, 'turn_q', 'proj'],
    [5, 'max0', 'score'],
    [5, 'selfY', 'self'],
    [6, 'selfV', 'self'],
    [6, 'self_max', 'self'],
    [8, 'max1', 'score'],
    [9, 'selfPT', 'self'],
    [10, 'natural0', 'late'],
    [10, 'natural1', 'late'],
    [12, 'attT', 'late'],
    [12, 'add_self', 'self'],
    [12, 'max2', 'score'],
    [13, 'wo', 'late'],
    [13, 'moments_ahead', 'any'],
    [15, 'normal_ahead', 'any'],
]
TAIL_DVE_WORK = [
    [0, 'max3', 'late'],
    [0, 'x3T', 'ffn'],
    [0, 'ctxT', 'proj'],
    [1, 'x2T', 'proj'],
    [2, 'turn_k', 'proj'],
    [2, 'gate_logits', 'ffn'],
    [3, 'turn_q', 'proj'],
    [5, 'max0', 'score'],
    [5, 'gate_weights', 'ffn'],
    [6, 'gates_low', 'ffn'],
    [7, 'gate0', 'ffn'],
    [7, 'gate1', 'ffn'],
    [7, 'low0', 'ffn'],
    [7, 'gate2', 'ffn'],
    [7, 'low1', 'ffn'],
    [7, 'gate3', 'ffn'],
    [8, 'max1', 'score'],
    [8, 'low2', 'ffn'],
    [8, 'low3', 'ffn'],
    [10, 'natural0', 'late'],
    [10, 'natural1', 'late'],
    [11, 'attT', 'late'],
    [12, 'max2', 'score'],
    [13, 'wo', 'late'],
    [13, 'moments_ahead', 'any'],
    [15, 'normal_ahead', 'any'],
    [15, 'out', 'ffn'],
]


def active(s):
    return [g for g in LAG if 0 <= s - LAG[g] < B]


def tables(s):
    if s < FULL_FROM:
        return HEAD_WORK, HEAD_ACT_WORK, HEAD_DVE_WORK
    if s >= FULL_TO:
        return TAIL_WORK, TAIL_ACT_WORK, TAIL_DVE_WORK
    return WORK, ACT_WORK, DVE_WORK


def uses_before(s, name):
    k = BANK[name]
    n = 0
    for step in range(s + 1):
        for _, other, stage in tables(step)[0]:
            if BANK[other] == k and stage in active(step):
                n += 1
            if step == s and other == name:
                return n


class Step:

    def __init__(self, s, round=None):
        self.s, self.round = s, round
        self.stages = active(s)

    def has(self, stage):
        if stage == "any":
            return "self" in self.stages or "late" in self.stages
        return stage in self.stages

    def batch(self, stage):
        b = self.s - LAG[stage]
        return b if self.round is None else self.round * 2 + b

    def parity(self, stage):
        return (self.s - LAG[stage]) % 2

    def number(self, per_step, done):
        n = per_step * self.s + done
        return n if self.round is None else self.round * (2 * per_step) + n

    def count(self, stage, per_batch, done):
        n = per_batch * (self.s - LAG[stage]) + done
        return n if self.round is None else self.round * (2 * per_batch) + n

    def turn(self, name, steps_ago=0):
        s = self.s - steps_ago
        n = uses_before(s, name)
        if self.round is None:
            return n
        return self.round * (uses_before(s + 2, name) - n) + n


LN_COLUMNS = (slice(0, 2), slice(2, 8))
LN_CALLS = (lambda st: lambda per_pass, done: st.count("self", per_pass, done),
            lambda st: st.number)


def wait(engine, semaphore, value):
    if isinstance(value, int) and value <= 0:
        return
    engine.wait_ge(semaphore, value)


def decoder_layer(nc, x, ctx, mask, Wq, Wk, Wv, wq, wk, wv, wo, w1, b1, w2, b2, cent, route,
                  c_ident, c_onehot, c_cos, c_sin, out):
    with ExitStack() as stack:
        def sb(name, shape, dt=F32):
            return stack.enter_context(nc.sbuf_tensor(name, shape, dt))

        def parts(name, shape):
            return sb(name + "_hi", shape, F32R), sb(name + "_lo", shape, F32R)

        def bank(name):
            return stack.enter_context(nc.psum_tensor(name, [P, 2, 256], F32))

        def sem(name):
            return stack.enter_context(nc.semaphore(name))

        scores_ps = [bank("scores0_ps"), bank("scores1_ps")]
        scoresT_ps = [bank("scoresT0_ps"), bank("scoresT1_ps")]
        pv_ps = bank("pv_ps")
        work_ps = [bank(f"work{k}_ps") for k in range(NBANKS)]

        parts_dram = nc.dram_tensor("parts", (2, 2, 2, P, C, S), F32).ap()

        ident = sb("ident", [P, P])
        ident_b = sb("ident_b", [P, P], BF16)
        cos_k = sb("cos_k", [P, S])
        sin_k = sb("sin_k", [P, S])
        cos_q = sb("cos_q", [P, S])
        sin_q = sb("sin_q", [P, S])
        onehot = sb("onehot", [QROWS, E, P], F32R)
        wqk = parts("wqk", [P, C, D])
        wT = parts("wT", [P, 5, C, D])
        w1s = parts("w1s", [P, C, E, DE])
        w2s = parts("w2s", [P, E, D])
        b1T = sb("b1T", [P, E])
        b2s = sb("b2s", [QROWS, D], F32R)
        cwT = parts("cwT", [P, C, 2 * E])
        cst = sb("cst", [E, 8])
        maskN = sb("maskN", [P, T, S])
        maskT = sb("maskT", [P, T, S], BF16)
        alive = sb("alive", [P, T])
        dead = sb("dead", [P, T])
        zero_col = sb("zero_col", [P, 1])
        carrier = sb("carrier", [P, 7])
        half_c = sb("half_c", [P, 8])
        three_c = sb("three_c", [P, 8])
        sixteenth_c = sb("sixteenth_c", [P, T])
        power_c = sb("power_c", [P, 8])

        xr = sb("xr", [P, RING, T, D])
        ctx_in = sb("ctx_in", [P, T, D])

        stats = sb("stats", [P, 6, 6])
        mv = sb("mv", [P, 8, 2])
        rs0 = sb("rs0", [P, 8])
        nw = sb("nw", [P, 4, 8])
        rstd = sb("rstd", [P, 8])
        cosn = sb("cosn", [P, 4, T])
        xT = parts("xT", [P, C, S])
        selfY = parts("selfY", [P, C, S])
        selfV = parts("selfV", [P, T, D])
        self_max = sb("self_max", [P, T])
        self_bias = sb("self_bias", [P, T])
        self_sum = sb("self_sum", [P, T])
        self_rec = sb("self_rec", [P, T])
        self_p = sb("self_p", [P, T, S])
        xn_stream = sb("xn_stream", [P, T, D])
        xn = [xn_stream, xn_stream, self_p]
        self_pT = selfY
        ctxT = parts("ctxT", [P, C, S])
        x2T = parts("x2T", [P, C, S])
        rope_hi = [sb("rope_hi_k", [P, C, S], F32R), sb("rope_hi_q", [P, C, S], F32R)]
        rope_lo = [sb("rope_lo_k", [P, C, S], F32R), sb("rope_lo_q", [P, C, S], F32R)]
        rope_a = [t[:].bitcast(F32) for t in rope_lo]
        rope_b = [sb("rope_b_k", [P, C, S]), sb("rope_b_q", [P, C, S])]
        kstack = sb("kstack", [P, H, S], F32R)
        qstack = sb("qstack", [P, H, S], F32R)
        vals = [sb("vals0", [P, T, H, VW]), sb("vals1", [P, T, H, VW])]
        maxima = sb("maxima", [P, T, H])
        mrow_hi = sb("mrow_hi", [4, 2, S], F32R)
        mrow_lo = sb("mrow_lo", [4, 2, S], F32R)
        probs = sb("probs", [P, NPROBS, T, S])
        att = sb("att", [P, 4, S])
        att_rec = sb("att_rec", [P, T, H])
        att_n = self_p
        attT = x2T
        x3T = parts("x3T", [P, C, S])
        logits_s = sb("logits_s", [P, S])
        logits2 = sb("logits2", [P, T, 2 * E])
        logit = sb("logit", [P, T, E])
        top = sb("top", [P, T, 8])
        shifted = sb("shifted", [P, T, E])
        expd = sb("expd", [P, T, E])
        kept = sb("kept", [P, T, E])
        ksum = sb("ksum", [P, T])
        krec = sb("krec", [P, T])
        gates = sb("gates", [P, T, QROWS])
        gatesT = sb("gatesT", [QROWS, S], F32R)
        hidden = sb("hidden", [P, 4, S])
        gated = parts("gated", [P, E, S])
        raw = ([hidden[:, 2 * i:2 * i + 2] for i in range(2)] + [t[:] for t in rope_b]
               + [probs[:, i] for i in range(3)])
        raw_experts = hidden[:]
        raw_mask = probs[:, 3].bitcast(I32)
        onehot_f = att[0:QROWS]
        raw_b2 = xr[0:QROWS, RING - 1, 0]
        csq = xr[0:E, RING - 2, 0]
        raw_b = xr[0:E, RING - 1, 1, 0:DE]
        raw_r = self_p[0:32 + E, 1]
        alive_b = self_p[:, 0].rearrange("p (t m) -> p t m", t=T)

        consts_loaded = sem("consts_loaded")
        ident_loaded = sem("ident_loaded")
        mask_loaded = sem("mask_loaded")
        weight_loaded = [sem(f"{name}_loaded") for name in ("Wq", "Wk", "Wv", "wq", "wk", "wv", "wo")]
        experts_loaded = sem("experts_loaded")
        small_loaded = sem("small_loaded")
        b2_loaded = sem("b2_loaded")
        x_loaded = [sem(f"x_loaded{i}") for i in range(len(PARTS))]
        x_ahead = [sem("x_ahead_even"), sem("x_ahead_odd")]
        ctx_loaded = sem("ctx_loaded")
        b2_zeroed = sem("b2_zeroed")
        small_set = sem("small_set")
        stacks_set = sem("stacks_set")
        buffers_set = sem("buffers_set")
        constants_made = sem("constants_made")
        cent_square = sem("cent_square")
        cent_newton = sem("cent_newton")
        setup_rounded = sem("setup_rounded")
        experts_rounded = sem("experts_rounded")
        experts_split = sem("experts_split")
        setup_formed = sem("setup_formed")
        setup_copied = sem("setup_copied")
        work_ready = [sem(f"work{k}_ready") for k in range(NBANKS)]
        work_copied = [sem(f"work{k}_copied") for k in range(NBANKS)]
        ln_stats = [sem("ln_stats_self"), sem("ln_stats_ahead")]
        ln_moments = [sem("ln_moments_self"), sem("ln_moments_ahead")]
        ln_var = [sem("ln_var_self"), sem("ln_var_ahead")]
        ln_power = [sem("ln_power_self"), sem("ln_power_ahead")]
        ln_newton = [sem("ln_newton_self"), sem("ln_newton_ahead")]
        xn_ready = [sem("xn_ready_self"), sem("xn_ready_proj"), sem("xn_ready_ffn")]
        cosn_ready = sem("cosn_ready")
        self_max_found = sem("self_max_found")
        self_bias_ready = sem("self_bias_ready")
        self_rec_ready = sem("self_rec_ready")
        rope_mixed = [sem("rope_mixed_k"), sem("rope_mixed_q")]
        rope_summed = [sem("rope_summed_k"), sem("rope_summed_q")]
        rope_rounded = [sem("rope_rounded_k"), sem("rope_rounded_q")]
        rope_split = [sem("rope_split_k"), sem("rope_split_q")]
        parts_saved = [sem("k_parts_saved"), sem("q_parts_saved")]
        stacked = [sem(f"stacked{g}") for g in range(4)]
        scores_ready = sem("scores_ready")
        max_found = sem("max_found")
        mrow_rounded = sem("mrow_rounded")
        mrow_loaded = [sem(f"mrow_loaded{g}") for g in range(4)]
        scoresT_ready = sem("scoresT_ready")
        probs_ready = sem("probs_ready")
        pv_done = sem("pv_done")
        att_copied = sem("att_copied")
        att_rec_ready = sem("att_rec_ready")
        gate_logit = sem("gate_logit")
        gate_top = sem("gate_top")
        gate_shift = sem("gate_shift")
        gate_exp = sem("gate_exp")
        gate_kept = sem("gate_kept")
        gate_rec = sem("gate_rec")
        gates_ready = sem("gates_ready")
        gated_rounded = sem("gated_rounded")
        gated_split = sem("gated_split")
        rounded = {name: sem(f"{name}_rounded") for name in SPLIT}
        gatesT_rounded = sem("gatesT_rounded")
        stored = sem("stored")

        def W(name):
            return work_ps[BANK[name]]

        def begin(pe, st, name):
            wait(pe, work_copied[BANK[name]], st.turn(name) - 1)

        def ready(engine, st, name):
            engine.wait_ge(work_ready[BANK[name]], st.turn(name))

        def copied(engine, st, name, steps_ago=0):
            engine.wait_ge(work_copied[BANK[name]], st.turn(name, steps_ago))

        def setup_parts(i):
            src = setup_banks[i % 4]
            if i == 0:
                return src[:], [t[:] for t in wqk]
            if i <= 5:
                return src[:], [t[:, i - 1] for t in wT]
            pairs = src[:, :, 0:64].rearrange("p c (a e) -> p c a e", a=2)[:, :, :, 0:E]
            return pairs, [t[:].rearrange("p c (a e) -> p c a e", a=2) for t in cwT]

        def experts_part(s, part):
            if s < 2:
                return w1s[part][:, s].rearrange("p e j -> p (e j)")
            return w2s[part][:, 4 * (s - 2):4 * (s - 1)].rearrange("p e d -> p (e d)")

        def rows(t, b):
            return t[:, b] if isinstance(b, int) else t[:, bass.ds(b, 1)].squeeze(1)

        def stream(b):
            return xr[:, b % RING] if isinstance(b, int) else xr[:, bass.ds(b & (RING - 1), 1)].squeeze(1)

        def run(engine, step):
            for s in range(FULL_FROM):
                if s == 1:
                    engine.wait_ge(buffers_set, BUFFERS_SET)
                if s == 2:
                    engine.wait_ge(stacks_set, STACKS_SET)
                step(Step(s))
            with engine.Fori(0, (FULL_TO - FULL_FROM) // 2) as r:
                for u in range(2):
                    step(Step(FULL_FROM + u, r))
            for s in range(FULL_TO, STEPS):
                step(Step(s))

        parts_of = {"ctxT": ctxT, "x3T": x3T, "x2T": x2T, "xT": xT, "selfY": selfY, "selfV": selfV,
                    "selfPT": self_pT, "attT": attT}
        setup_banks = scores_ps + scoresT_ps

        block = stack.enter_context(nc.Block())

        @block.sync
        def _(sp):
            xv = x.rearrange("b (t p) d -> p b t d", p=P)
            cv = ctx.rearrange("b (t p) d -> p b t d", p=P)

            def load(i):
                lo, hi = PARTS[i]
                sp.dma_start(xr[:, lo:hi], xv[:, lo:hi]).then_inc(x_loaded[i], 16)

            sources = (Wq, Wk, Wv, wq, wk, wv, wo)
            for i, w in enumerate(sources[:2]):
                sp.dma_start(raw[i], w.rearrange("(c p) d -> p c d", p=P)).then_inc(weight_loaded[i], 16)
            sp.dma_start(ident[:], c_ident).then_inc(ident_loaded, 16)
            sp.dma_start(raw_mask, mask.rearrange("a b (t p) k -> p (a b t) k", p=P)).then_inc(mask_loaded, 16)
            sp.dma_start(raw[2], Wv.rearrange("(c p) d -> p c d", p=P)).then_inc(weight_loaded[2], 16)
            load(0)
            sp.dma_start(raw_r[0:E], cent).then_inc(small_loaded, 16)
            sp.dma_start(raw_r[32:32 + E], route).then_inc(small_loaded, 16)
            for i in range(3, len(sources)):
                sp.dma_start(raw[i], sources[i].rearrange("(c p) d -> p c d", p=P)).then_inc(weight_loaded[i], 16)
            sp.dma_start(raw_b, b1).then_inc(small_loaded, 16)
            for dst, src in ((cos_k[:], c_cos), (sin_k[:], c_sin),
                             (onehot_f.rearrange("p a b -> p (a b)"), c_onehot)):
                sp.dma_start(dst, src).then_inc(consts_loaded, 16)
            sp.wait_ge(b2_zeroed, 1)
            for i in range(3):
                sp.dma_start(raw_b2[32 * i:32 * i + E], b2).then_inc(b2_loaded, 16)
            for i in range(1, len(PARTS)):
                load(i)
            outv = out.rearrange("b (t p) d -> p b t d", p=P)

            def load_context(st):
                if st.has("proj"):
                    copied(sp, st, "ctxT")
                sp.dma_start(ctx_in[:], rows(cv, st.batch("self"))).then_inc(ctx_loaded, 16)

            def load_experts(s):
                if s == 0:
                    sp.wait_ge(setup_copied, SETUP)
                wait(sp, experts_split, s)
                if s < 2:
                    src = w1[:, s * P:(s + 1) * P, :].rearrange("e p j -> p e j")
                else:
                    src = w2[4 * (s - 2):4 * (s - 1)].rearrange("e j d -> j e d")
                sp.dma_start(raw_experts.rearrange("p a b -> p (a b)").rearrange("p (e j) -> p e j", e=src.shape[1]),
                             src).then_inc(experts_loaded, 16)

            def load_next(st):
                b = st.batch("self") + 1
                source = xv[:, b % B] if isinstance(b, int) else xv[:, bass.ds(b & (B - 1), 1)].squeeze(1)
                sp.dma_start(stream(b), source).then_inc(x_ahead[(st.s + 1) % 2], 16)

            def send_maxima(st, stage, g):
                copied(sp, st, f"max{g}")
                for row, src in ((QROWS, mrow_hi), (QROWS + 1, mrow_lo)):
                    if g == 0 and row > QROWS and st.s >= FULL_FROM and st.has("self"):
                        sp.wait_ge(stored, st.number(16, 1 - 16 * LAST_LAG))
                    sp.dma_start(qstack[row:row + 1, 4 * g:4 * g + 4, :].bitcast(F32),
                                 src[:, g % 2, :].bitcast(F32)).then_inc(mrow_loaded[g], 16)

            def save_parts(st, j):
                if j == 0:
                    wait(sp, stacked[3], st.count("proj", STACKED, -STACKED))
                sp.wait_ge(rope_split[j], st.count("proj", 1, 1))
                for k, src in enumerate((rope_hi[j], rope_lo[j])):
                    if j == 1 and k == 1:
                        sp.wait_ge(parts_saved[0], st.count("proj", 32, 32))
                    sp.dma_start(parts_dram[st.parity("proj"), j, k], src[:].bitcast(F32)).then_inc(parts_saved[j], 16)

            def stack_heads(st, stage, g):
                wait(sp, scoresT_ready, st.count(stage, H, 4 * g + 4 - H))
                c, h0 = 4 * g // HC, 4 * g % HC
                for j, stack_ in enumerate((kstack, qstack)):
                    if g == 0 and j == 1:
                        sp.wait_ge(parts_saved[1], st.count(stage, 32, 32))
                    for r in range(3):
                        part = 1 if r == 1 + j else 0
                        src = parts_dram[st.parity(stage), j, part, DK * h0:DK * (h0 + 4), c]
                        sp.dma_start(stack_[DK * r:DK * r + DK, 4 * g:4 * g + 4, :].bitcast(F32),
                                     src.rearrange("(h d) t -> d h t", d=DK)).then_inc(stacked[g], 16)

            def step(st):
                if st.has("self"):
                    load_context(st)
                if st.round is None and st.s < 4:
                    load_experts(st.s)
                if st.s == 1:
                    sp.wait_ge(stacks_set, STACKS_SET)
                if st.has("late"):
                    send_maxima(st, "late", 3)
                if st.has("score"):
                    stack_heads(st, "score", 2)
                    send_maxima(st, "score", 0)
                if st.has("self") and st.s >= FULL_FROM - 1:
                    load_next(st)
                if st.has("proj"):
                    save_parts(st, 0)
                if st.has("score"):
                    stack_heads(st, "score", 3)
                    send_maxima(st, "score", 1)
                if st.has("proj"):
                    save_parts(st, 1)
                    stack_heads(st, "proj", 0)
                if st.has("score"):
                    send_maxima(st, "score", 2)
                if st.has("proj"):
                    stack_heads(st, "proj", 1)
                if st.has("ffn"):
                    copied(sp, st, "out")
                    b = st.batch("ffn")
                    sp.dma_start(rows(outv, b), stream(b)).then_inc(stored, 16)

            run(sp, step)
            sp.wait_ge(stored, 16 * B + 1)
            sp.wait_ge(x_ahead[0], 16 * ((B - FULL_FROM) // 2 + 1))

        @block.gpsimd
        def _(pool):
            g = nc.gpsimd
            g.memset(raw_b2, 0.0).then_inc(b2_zeroed, 1)
            g.memset(carrier[:, 6:7], 0.0).then_inc(stored, 1)
            for t, value in ((half_c, 0.5), (three_c, 3.0), (sixteenth_c, 1.0 / 16.0), (power_c, -0.5), (mv, 1.0),
                             (gates, 0.0), (logits_s, 0.0)):
                g.memset(t[:], value).then_inc(small_set, 1)
            pool.wait_ge(small_set, SMALL_SET)

            pool.wait_ge(cent_square, 2)
            g.tensor_tensor(cst[:, 2:3], cst[:, 0:1], power_c[0:E, 0:1], ALU.pow).then_inc(cent_newton, 1)
            pool.wait_ge(cent_newton, 1)
            g.tensor_tensor(cst[:, 3:4], cst[:, 2:3], cst[:, 2:3], ALU.mult).then_inc(cent_newton, 1)
            pool.wait_ge(cent_newton, 2)
            g.tensor_tensor(cst[:, 4:5], cst[:, 3:4], cst[:, 0:1], ALU.mult).then_inc(cent_newton, 1)
            pool.wait_ge(cent_newton, 3)
            g.tensor_scalar(cst[:, 5:6], cst[:, 4:5], -0.5, 1.5, ALU.mult, ALU.add).then_inc(cent_newton, 1)
            pool.wait_ge(cent_newton, 4)
            g.tensor_tensor(cst[:, 6:7], cst[:, 5:6], cst[:, 2:3], ALU.mult).then_inc(cent_newton, 1)

            def newton(st, group):
                k = LN_COLUMNS[group]
                n = LN_CALLS[group](st)
                pool.wait_ge(ln_var[group], n(1, 1))
                g.tensor_tensor(rs0[:, k], mv[:, k, 1], power_c[:, k], ALU.pow).then_inc(ln_power[group], 1)
                pool.wait_ge(ln_power[group], n(1, 1))
                g.tensor_tensor(nw[:, 0, k], rs0[:, k], rs0[:, k], ALU.mult)
                g.tensor_tensor(nw[:, 3, k], rs0[:, k], half_c[:, k], ALU.mult).then_inc(ln_newton[group], 1)
                pool.wait_ge(ln_newton[group], n(4, 1))
                g.tensor_tensor(nw[:, 1, k], nw[:, 0, k], mv[:, k, 1], ALU.mult).then_inc(ln_newton[group], 1)
                pool.wait_ge(ln_newton[group], n(4, 2))
                g.tensor_tensor(nw[:, 2, k], three_c[:, k], nw[:, 1, k], ALU.subtract).then_inc(ln_newton[group], 1)
                pool.wait_ge(ln_newton[group], n(4, 3))
                g.tensor_tensor(rstd[:, k], nw[:, 2, k], nw[:, 3, k], ALU.mult).then_inc(ln_newton[group], 1)

            def inverse_norm(st):
                pool.wait_ge(ln_newton[1], st.number(4, 4))
                g.tensor_tensor(cosn[:, 0], rstd[:, 6:8], rstd[:, 4:6], ALU.mult).then_inc(cosn_ready, 1)
                pool.wait_ge(cosn_ready, st.count("late", 3, 1))
                g.tensor_tensor(cosn[:, 1], cosn[:, 0], mv[:, 4:6, 1], ALU.mult).then_inc(cosn_ready, 1)
                pool.wait_ge(cosn_ready, st.count("late", 3, 2))
                g.tensor_tensor(cosn[:, 2], cosn[:, 1], sixteenth_c[:], ALU.mult).then_inc(cosn_ready, 1)

            def rope(st, j):
                sin = (sin_k, sin_q)[j]
                copied(pool, st, ("keys", "queries")[j])
                g.tensor_tensor(rope_b[j][:], rope_b[j][:], sin[:].unsqueeze(1).to_broadcast([P, C, S]),
                                ALU.mult).then_inc(rope_mixed[j], 1)
                pool.wait_ge(rope_mixed[j], st.count("proj", 1, 1))
                g.tensor_tensor(rope_a[j], rope_a[j], rope_b[j][:], ALU.add).then_inc(rope_summed[j], 1)
                pool.wait_ge(rope_rounded[j], st.count("proj", 1, 1))
                g.tensor_tensor(rope_lo[j][:], rope_a[j], rope_hi[j][:].bitcast(F32),
                                ALU.subtract).then_inc(rope_split[j], 1)

            def split_experts(s):
                pool.wait_ge(experts_rounded, s + 1)
                g.tensor_tensor(experts_part(s, 1), raw_experts.rearrange("p a b -> p (a b)"),
                                experts_part(s, 0).bitcast(F32), ALU.subtract).then_inc(experts_split, 1)

            def step(st):
                if st.has("self"):
                    newton(st, 0)
                if st.s == 0 and st.round is None:
                    for i in range(2):
                        g.memset(vals[i][:], 1.0).then_inc(buffers_set, 1)
                    g.memset(qstack[:].bitcast(F32), 0.0).then_inc(stacks_set, 1)
                    g.memset(kstack[:].bitcast(F32), 0.0).then_inc(stacks_set, 1)
                if st.has("proj"):
                    rope(st, 0)
                    rope(st, 1)
                if st.has("self") or st.has("late"):
                    newton(st, 1)
                if st.has("late"):
                    inverse_norm(st)
                if st.round is None and st.s < 4:
                    split_experts(st.s)
                if st.s == 0:
                    pool.wait_ge(stacks_set, 2)
                    pool.wait_ge(experts_split, 1)
                    g.memset(kstack[QROWS:MROWS].bitcast(F32), -1.0).then_inc(stacks_set, 1)
                    pool.wait_ge(stacks_set, 3)

            run(pool, step)

        @block.scalar
        def _(act):
            a = nc.scalar
            a.preload_act_table(ACT.Exp)
            for i in range(7):
                act.wait_ge(setup_formed, i + 1)
                src, (hi, lo) = setup_parts(i)
                a.copy(hi, src).then_inc(setup_rounded, 1)
            act.wait_ge(consts_loaded, 48)
            a.copy(onehot[:], onehot_f.rearrange("p a b -> p (a b)").rearrange("p (e j) -> p e j", e=E)).then_inc(
                buffers_set, 1)

            def copy_out(st, name, dst, src=None):
                ready(act, st, name)
                a.copy(dst, W(name)[:] if src is None else src).then_inc(work_copied[BANK[name]], 1)

            def round_out(st, name):
                ready(act, st, name)
                a.copy(parts_of[name][0][:], W(name)[:]).then_inc(rounded[name], 1)

            def round_experts(s):
                act.wait_ge(experts_loaded, 16 * (s + 1))
                a.copy(experts_part(s, 0), raw_experts.rearrange("p a b -> p (a b)")).then_inc(experts_rounded, 1)

            def round_gated(st, i):
                copied(act, st, f"gate{i}")
                k = 2 * i % 4
                a.copy(gated[0][:, 2 * i:2 * i + 2], hidden[:, k:k + 2]).then_inc(gated_rounded, 1)

            def softmax(st, stage, h):
                act.wait_ge(scoresT_ready, st.count(stage, H, h + 1))
                wait(act, pv_done, st.count(stage, H, h + 1 - NPROBS))
                a.activation(probs[:, h % NPROBS], scoresT_ps[h % 2][:], ACT.Exp, bias=zero_col[:],
                             scale=INV_SQRT_DK).then_inc(probs_ready, 1)

            def copy_attention(st, half):
                act.wait_ge(pv_done, st.count("late", H, 8 * half + 8))
                a.copy(att[:, 2 * half:2 * half + 2, :], pv_ps[:]).then_inc(att_copied, 1)

            def rope_round(st, j):
                act.wait_ge(rope_summed[j], st.count("proj", 1, 1))
                a.copy(rope_hi[j][:], rope_a[j]).then_inc(rope_rounded[j], 1)

            def expert_rows(st, i):
                name = f"hidden{i}"
                if i >= 2:
                    act.wait_ge(gated_split, st.count("ffn", 4, i - 1))
                ready(act, st, name)
                for k in range(2):
                    e = 2 * i + k
                    last = a.activation(hidden[:, e % 4], W(name)[:, k], ACT.Gelu, bias=b1T[:, e:e + 1])
                last.then_inc(work_copied[BANK[name]], 1)

            def gate_exponentials(st):
                act.wait_ge(gate_shift, st.count("ffn", 1, 1))
                a.activation(expd[:], shifted[:], ACT.Exp, bias=zero_col[:]).then_inc(gate_exp, 1)

            def gates_out(st):
                ready(act, st, "gatesT")
                a.copy(gatesT[:], W("gatesT")[0:QROWS, 0, :]).then_inc(gatesT_rounded, 1)

            def self_softmax(st):
                act.wait_ge(self_bias_ready, st.count("self", 1, 1))
                for t in range(T):
                    last = a.activation(self_p[:, t], W("selfS")[:, t], ACT.Exp, bias=self_bias[:, t:t + 1],
                                        scale=INV_SQRT_D, accum_out=self_sum[:, t:t + 1])
                last.then_inc(work_copied[BANK["selfS"]], 1)

            actions = {
                "attention0": lambda st: copy_attention(st, 0),
                "attention1": lambda st: copy_attention(st, 1),
                "logits": lambda st: copy_out(st, "logits", logits_s[0:2 * E, :], W("logits")[0:2 * E, 0, :]),
                "round_k": lambda st: rope_round(st, 0),
                "round_q": lambda st: rope_round(st, 1),
                "gate_exp": gate_exponentials,
                "softmax": self_softmax,
                "gatesT": gates_out,
                "gelu0": lambda st: expert_rows(st, 0),
                "gelu1": lambda st: expert_rows(st, 1),
                "gelu2": lambda st: expert_rows(st, 2),
                "gelu3": lambda st: expert_rows(st, 3),
                "values": lambda st: copy_out(st, "values", vals[st.parity("proj")][:, :, :, 0:DK],
                                              W("values")[:].rearrange("p t (h d) -> p t h d", h=H)),
                "gated0": lambda st: round_gated(st, 0),
                "gated1": lambda st: round_gated(st, 1),
                "gated2": lambda st: round_gated(st, 2),
                "gated3": lambda st: round_gated(st, 3),
            }

            def step(st):
                for h in range(H):
                    if h < 8 and st.has("late"):
                        softmax(st, "late", h + 8)
                    if h >= 8 and st.has("score"):
                        softmax(st, "score", h - 8)
                    for slot, name, stage in tables(st.s)[1]:
                        if slot == h and st.has(stage):
                            if name in SPLIT:
                                round_out(st, name)
                            else:
                                actions[name](st)
                if st.round is None and st.s < 4:
                    round_experts(st.s)

            run(act, step)

        @block.vector
        def _(dve):
            v = nc.vector
            made = [0]

            def chain(ins):
                made[0] += 1
                ins.then_inc(constants_made, 1)
                dve.wait_ge(constants_made, made[0])

            def carry(i):
                v.memset(carrier[:, i:i + 1], 0.0)

            def moments(st, group):
                n = LN_CALLS[group](st)
                if group == 0:
                    for i, (lo, hi) in enumerate(PARTS):
                        if st.s == lo:
                            dve.wait_ge(x_loaded[i], 16)
                    if st.round is not None:
                        dve.wait_ge(x_ahead[st.s % 2], st.round * 16 + 16)
                    parts = [(0, "self")]
                else:
                    parts = [(1, "self")] * st.has("self") + [(2, "late")] * st.has("late")
                    carry(5)
                for i, stage in parts:
                    x_rows = stream(st.batch(stage))
                    for t in range(T):
                        last = v.bn_stats(stats[:, 2 * i + t], x_rows[:, t])
                last.then_inc(ln_stats[group], 1)
                dve.wait_ge(ln_stats[group], n(1, 1))
                carry(2 if group else 4)
                for i, _ in parts:
                    for t in range(T):
                        last = v.bn_aggr(mv[:, 2 * i + t], stats[:, 2 * i + t])
                last.then_inc(ln_moments[group], 1)
                dve.wait_ge(ln_moments[group], n(1 + group, 1))
                if group == 1:
                    v.tensor_scalar(mv[:, 6:8, 1], mv[:, 4:6, 1], 1e-37, None, ALU.max).then_inc(ln_moments[group], 1)
                    dve.wait_ge(ln_moments[group], n(2, 2))
                k = slice(0, 2) if group == 0 else slice(2, 6)
                v.tensor_scalar(mv[:, k, 1], mv[:, k, 1], EPS, None, ALU.add).then_inc(ln_var[group], 1)

            def normalise(st, group, i, stage):
                dve.wait_ge(ln_newton[group], LN_CALLS[group](st)(4, 4))
                x_rows = stream(st.batch(stage))
                for t in range(T):
                    k = 2 * i + t
                    last = v.tensor_scalar(xn[i][:, t], x_rows[:, t], mv[:, k, 0:1], rstd[:, k:k + 1],
                                           ALU.subtract, ALU.mult)
                last.then_inc(xn_ready[i], 1)

            chain(v.memset(zero_col[:], 0.0))
            dve.wait_ge(ident_loaded, 16)
            v.tensor_copy(ident_b[:], ident[:]).then_inc(setup_copied, 1)
            dve.wait_ge(mask_loaded, 16)
            chain(v.tensor_scalar(maskN[:], raw_mask, 0.0, None, ALU.not_equal))
            chain(v.tensor_reduce(alive[:], maskN[:], AX_X, ALU.max))
            chain(v.tensor_scalar(dead[:], alive[:], -1.0, 1.0, ALU.mult, ALU.add))
            for t in range(T):
                v.tensor_scalar(alive_b[:, t], ident[:], 0.0, alive[:, t:t + 1], ALU.mult, ALU.add)
                chain(v.tensor_scalar(maskN[:, t], maskN[:, t], dead[:, t:t + 1], 1.0, ALU.max, ALU.subtract))
            chain(v.tensor_scalar(maskN[:], maskN[:], -MASKED, None, ALU.mult))
            for i in range(SETUP - 1):
                if i == 1:
                    dve.wait_ge(small_loaded, 48)
                    v.tensor_tensor_reduce(csq, raw_r[0:E], raw_r[0:E], 1.0, 0.0, ALU.mult, ALU.add,
                                           cst[:, 7:8]).then_inc(cent_square, 1)
                    dve.wait_ge(cent_square, 1)
                    v.tensor_scalar(cst[:, 0:1], cst[:, 7:8], 1e-24, None, ALU.max).then_inc(cent_square, 1)
                if i == 2:
                    dve.wait_ge(small_set, SMALL_SET)
                    moments(Step(0), 0)
                if i == 3:
                    dve.wait_ge(cent_newton, 5)
                    chain(v.tensor_scalar(raw_r[0:E], raw_r[0:E], cst[:, 6:7], None, ALU.mult))
                dve.wait_ge(setup_formed, i + 1)
                src = setup_banks[i % 4]
                if i <= 6:
                    dve.wait_ge(setup_rounded, i + 1)
                    src, (hi, lo) = setup_parts(i)
                    ins = v.tensor_tensor(lo, src, hi.bitcast(F32), ALU.subtract)
                elif i == 7:
                    ins = v.tensor_copy(b1T[:], src[:, 0, 0:E])
                elif i == 8:
                    dve.wait_ge(consts_loaded, 48)
                    v.tensor_tensor(cos_q[:], cos_k[:], src[:, 0, :], ALU.mult)
                    ins = v.tensor_tensor(sin_q[:], sin_k[:], src[:, 0, :], ALU.mult)
                else:
                    ins = v.tensor_copy(maskT[:], src[:])
                ins.then_inc(setup_copied, 1)
                if i == 5:
                    normalise(Step(0), 0, 0, "self")
            def split_out(st, name):
                dve.wait_ge(rounded[name], st.count(STAGE[name], 1, 1))
                hi, lo = parts_of[name]
                v.tensor_tensor(lo[:], W(name)[:], hi[:].bitcast(F32), ALU.subtract).then_inc(
                    work_copied[BANK[name]], 1)

            def head_max(st, h):
                dve.wait_ge(scores_ready, st.count("score", H, h + 1))
                carry(h % 2)
                for t in range(T):
                    s_ps = scores_ps[h % 2][:, t]
                    last = v.tensor_tensor_reduce(s_ps, s_ps, maskN[:, t], 1.0, LOWEST, ALU.add, ALU.max,
                                                  maxima[:, t, h:h + 1])
                last.then_inc(max_found, 1)

            def round_maxima(st, stage, g):
                name = f"max{g}"
                ready(dve, st, name)
                wait(dve, mrow_loaded[(g + 2) % 4], st.count(stage, 32, 32 if g >= 2 else 0))
                v.tensor_copy(mrow_hi[:, g % 2], W(name)[0:4, 0, :]).then_inc(mrow_rounded, 1)
                dve.wait_ge(mrow_rounded, st.count(stage, 4, g + 1))
                v.tensor_tensor(mrow_lo[:, g % 2], W(name)[0:4, 0, :], mrow_hi[:, g % 2].bitcast(F32),
                                ALU.subtract).then_inc(work_copied[BANK[name]], 1)

            def turn_pairs(st, j):
                name = ("keys", "queries")[j]
                ready(dve, st, name)
                cos = (cos_k, cos_q)[j]
                wait(dve, parts_saved[j], st.count("proj", 32, 0))
                v.tensor_tensor(rope_a[j], W(name)[:], cos[:].unsqueeze(1).to_broadcast([P, C, S]), ALU.mult)
                v.stream_shuffle(rope_b[j][:], W(name)[:], [i ^ 1 for i in range(32)]).then_inc(
                    work_copied[BANK[name]], 1)

            def self_maximum(st):
                ready(dve, st, "selfS")
                v.tensor_reduce(self_max[:], W("selfS")[:], AX_X, ALU.max).then_inc(self_max_found, 1)
                dve.wait_ge(self_max_found, st.count("self", 1, 1))
                v.tensor_scalar(self_bias[:], self_max[:], -INV_SQRT_D, None, ALU.mult).then_inc(self_bias_ready, 1)

            def add_self_attention(st):
                copied(dve, st, "selfS")
                v.reciprocal(self_rec[:], self_sum[:]).then_inc(self_rec_ready, 1)
                dve.wait_ge(self_rec_ready, st.count("self", 1, 1))
                ready(dve, st, "selfO")
                x_rows = stream(st.batch("self"))
                for t in range(T):
                    last = v.scalar_tensor_tensor(x_rows[:, t], W("selfO")[:, t], self_rec[:, t:t + 1], x_rows[:, t],
                                                  ALU.mult, ALU.add)
                last.then_inc(work_copied[BANK["selfO"]], 1)

            def add_to_stream(st, name, stage):
                ready(dve, st, name)
                x_rows = stream(st.batch(stage))
                v.tensor_tensor(x_rows, x_rows, W(name)[:], ALU.add).then_inc(work_copied[BANK[name]], 1)

            def normalise_attention(st, t):
                name = f"natural{t}"
                ready(dve, st, name)
                heads = W(name)[:].rearrange("p a (g w) -> p (a g) w", w=VW)
                v.reciprocal(att_rec[:, t], heads[:, :, DK]).then_inc(att_rec_ready, 1)
                dve.wait_ge(att_rec_ready, st.count("late", T, t + 1))
                v.tensor_tensor(att_n[:, t].rearrange("p (h d) -> p h d", h=H), heads[:, :, 0:DK], att_rec[:, t].unsqueeze(2).to_broadcast([P, H, DK]),
                                ALU.mult).then_inc(work_copied[BANK[name]], 1)

            def gate_logits(st):
                dve.wait_ge(cosn_ready, st.count("ffn", 3, 3))
                ready(dve, st, "logitsT")
                v.tensor_scalar(cosn[:, 3], cosn[:, 2], NORM_MAX, None, ALU.min)
                v.tensor_copy(logits2[:], W("logitsT")[:, 0].rearrange("p (t e) -> p t e", t=T)[:, :, 0:2 * E]).then_inc(
                    work_copied[BANK["logitsT"]], 1)
                copied(dve, st, "logitsT")
                for t in range(T):
                    last = v.scalar_tensor_tensor(logit[:, t], logits2[:, t, 0:E], cosn[:, 3, t:t + 1],
                                                  logits2[:, t, E:2 * E], ALU.mult, ALU.add)
                last.then_inc(gate_logit, 1)
                dve.wait_ge(gate_logit, st.count("ffn", 1, 1))
                carry(3)
                for t in range(T):
                    last = v.max(top[:, t], logit[:, t])
                last.then_inc(gate_top, 1)
                dve.wait_ge(gate_top, st.count("ffn", 1, 1))
                for t in range(T):
                    last = v.tensor_scalar(shifted[:, t], logit[:, t], top[:, t, 0:1], None, ALU.subtract)
                last.then_inc(gate_shift, 1)

            def gate_weights(st):
                dve.wait_ge(gate_exp, st.count("ffn", 1, 1))
                for t in range(T):
                    last = v.scalar_tensor_tensor(kept[:, t], logit[:, t], top[:, t, 1:2], expd[:, t],
                                                  ALU.is_ge, ALU.mult, accum_out=ksum[:, t:t + 1])
                last.then_inc(gate_kept, 1)
                dve.wait_ge(gate_kept, st.count("ffn", 1, 1))
                v.reciprocal(krec[:], ksum[:]).then_inc(gate_rec, 1)
                dve.wait_ge(gate_rec, st.count("ffn", 1, 1))
                for t in range(T):
                    last = v.tensor_scalar(gates[:, t].rearrange("p (r c) -> p r c", r=3)[:, :, 0:E],
                                           kept[:, t].unsqueeze(1).to_broadcast([P, 3, E]),
                                           krec[:, t:t + 1], None, ALU.mult)
                last.then_inc(gates_ready, 1)

            def gates_low_part(st):
                dve.wait_ge(gatesT_rounded, st.count("ffn", 1, 1))
                v.tensor_tensor(gatesT[32:32 + E], W("gatesT")[32:32 + E, 0, :], gatesT[32:32 + E].bitcast(F32),
                                ALU.subtract).then_inc(work_copied[BANK["gatesT"]], 1)

            def apply_gate(st, i):
                name = f"gate{i}"
                copied(dve, st, f"hidden{i}")
                ready(dve, st, name)
                k = 2 * i % 4
                v.tensor_tensor(hidden[:, k:k + 2], hidden[:, k:k + 2], W(name)[:], ALU.mult).then_inc(
                    work_copied[BANK[name]], 1)

            def low_gated(st, i):
                dve.wait_ge(gated_rounded, st.count("ffn", 4, i + 1))
                k, held = slice(2 * i, 2 * i + 2), slice(2 * i % 4, 2 * i % 4 + 2)
                v.tensor_tensor(gated[1][:, k], hidden[:, held], gated[0][:, k].bitcast(F32),
                                ALU.subtract).then_inc(gated_split, 1)

            def moments_ahead(st):
                if st.has("self"):
                    copied(dve, st, "selfO")
                if st.has("late"):
                    copied(dve, st, "wo")
                moments(st, 1)

            def normalise_ahead(st):
                if st.has("late"):
                    normalise(st, 1, 2, "late")
                if st.has("self"):
                    normalise(st, 1, 1, "self")

            actions = {
                "max3": lambda st: round_maxima(st, "late", 3),
                "max0": lambda st: round_maxima(st, "score", 0),
                "max1": lambda st: round_maxima(st, "score", 1),
                "max2": lambda st: round_maxima(st, "score", 2),
                "moments_self": lambda st: st.s > 0 and moments(st, 0),
                "normal_self": lambda st: st.s > 0 and normalise(st, 0, 0, "self"),
                "turn_k": lambda st: turn_pairs(st, 0),
                "turn_q": lambda st: turn_pairs(st, 1),
                "gate_logits": gate_logits,
                "gate_weights": gate_weights,
                "self_max": self_maximum,
                "gates_low": gates_low_part,
                "gate0": lambda st: apply_gate(st, 0),
                "gate1": lambda st: apply_gate(st, 1),
                "gate2": lambda st: apply_gate(st, 2),
                "gate3": lambda st: apply_gate(st, 3),
                "low0": lambda st: low_gated(st, 0),
                "low1": lambda st: low_gated(st, 1),
                "low2": lambda st: low_gated(st, 2),
                "low3": lambda st: low_gated(st, 3),
                "natural0": lambda st: normalise_attention(st, 0),
                "natural1": lambda st: normalise_attention(st, 1),
                "add_self": add_self_attention,
                "wo": lambda st: add_to_stream(st, "wo", "late"),
                "out": lambda st: add_to_stream(st, "out", "ffn"),
                "moments_ahead": moments_ahead,
                "normal_ahead": normalise_ahead,
            }

            def split_b2():
                dve.wait_ge(b2_loaded, 48)
                chain(v.tensor_copy(b2s[:], raw_b2))
                v.tensor_tensor(b2s[64:QROWS], raw_b2[64:QROWS], b2s[64:QROWS].bitcast(F32), ALU.subtract).then_inc(
                    buffers_set, 1)

            def step(st):
                for h in range(H):
                    if st.s == 0 and h == 5:
                        split_b2()
                    if st.has("score"):
                        head_max(st, h)
                    for slot, name, stage in tables(st.s)[2]:
                        if slot == h and st.has(stage):
                            if name in SPLIT:
                                split_out(st, name)
                            else:
                                actions[name](st)

            run(dve, step)

        @block.tensor
        def _(pe):
            t_ = nc.tensor

            def transposed(dst, src, fill=None):
                for c in range(C):
                    for t in range(T):
                        last = t_.transpose(dst[:, c, t * P:(t + 1) * P], src[:, t, c * P:(c + 1) * P], ident[:])
                return last

            def accumulate(dst, factors, first=True, final=True):
                terms = []
                for left, right in factors:
                    if len(left) == 1:
                        terms.append((left[0], right[0]))
                    else:
                        terms += [(left[0], right[0]), (left[0], right[1]), (left[1], right[0])]
                for i, (left, right) in enumerate(terms):
                    last = t_.matmul(dst, left, right, start=first and i == 0,
                                     stop=final and i == len(terms) - 1)
                return last

            def product(dst, left, right):
                for m in range(2):
                    last = accumulate(dst[:, m], [([l[:, c, m * P:(m + 1) * P] for l in left],
                                                   [r[:, c, :] for r in right]) for c in range(C)])
                return last

            def weight(i):
                return [t[:, i] for t in wT]

            pe.wait_ge(weight_loaded[0], 16)
            pe.wait_ge(weight_loaded[1], 16)
            for i in range(SETUP - 1):
                wait(pe, setup_copied, i - 3 + 1 if i > 3 else 0)
                dst = setup_banks[i % 4]
                if i == 0:
                    last = product(dst, [raw[0]], [raw[1]])
                elif i <= 5:
                    if i == 1:
                        pe.wait_ge(ident_loaded, 16)
                    pe.wait_ge(weight_loaded[1 + i], 16)
                    last = transposed(dst, raw[1 + i])
                elif i == 6:
                    pe.wait_ge(small_loaded, 48)
                    pe.wait_ge(constants_made, CENTROIDS_MADE)
                    for c in range(C):
                        last = t_.transpose(dst[:, c, 0:32 + E], raw_r[0:32 + E, c * P:(c + 1) * P],
                                            ident[0:32 + E, 0:32 + E])
                elif i == 7:
                    last = t_.transpose(dst[:, 0, 0:E], raw_b, ident[0:E, 0:E])
                elif i == 8:
                    for t in range(T):
                        last = t_.matmul(dst[:, 0, t * P:(t + 1) * P], alive_b[:, t], ident[:], start=True, stop=True)
                else:
                    last = transposed(dst, maskN[:])
                last.then_inc(setup_formed, 1)
            pe.wait_ge(setup_copied, SETUP)

            def finish(last, name):
                last.then_inc(work_ready[BANK[name]], 1)

            def scores(st, h):
                if h % 4 == 0:
                    pe.wait_ge(stacked[h // 4], st.count("score", STACKED, STACKED))
                wait(pe, max_found, st.count("score", H, h - 1))
                for t in range(T):
                    last = t_.matmul(scores_ps[h % 2][:, t], qstack[0:QROWS, h, t * P:(t + 1) * P],
                                     kstack[0:QROWS, h, :], start=True, stop=True)
                last.then_inc(scores_ready, 1)

            def scoresT(st, stage, h):
                if h % 4 == 0:
                    pe.wait_ge(mrow_loaded[h // 4], st.count(stage, 32, 32))
                wait(pe, probs_ready, st.count(stage, H, h - 1))
                for t in range(T):
                    t_.matmul(scoresT_ps[h % 2][:, t], kstack[0:MROWS, h, t * P:(t + 1) * P],
                              qstack[0:MROWS, h, :], start=True, stop=False)
                    last = t_.matmul(scoresT_ps[h % 2][:, t], ident_b[:], maskT[:, t], start=False, stop=True)
                last.then_inc(scoresT_ready, 1)

            def values_product(st, stage, h):
                par = st.parity(stage)
                pe.wait_ge(probs_ready, st.count(stage, H, h + 1))
                if h % 8 == 0:
                    wait(pe, att_copied, st.count(stage, 2, h // 8))
                j = h % 4
                for t in range(T):
                    last = t_.matmul(pv_ps[VW * j:VW * j + VW, h // 4 % 2], vals[par][:, t, h, :],
                                     probs[:, h % NPROBS, t], start=t == 0, stop=t == T - 1)
                last.then_inc(pv_done, 1)

            def work(st, name):
                begin(pe, st, name)
                ps = W(name)

                def need(other):
                    if BANK[other] != BANK[name]:
                        copied(pe, st, other)

                if name in ("xT", "x2T", "x3T"):
                    i = ("xT", "x2T", "x3T").index(name)
                    pe.wait_ge(xn_ready[i], st.count(STAGE[name], 1, 1))
                    last = transposed(ps, xn[i])
                elif name == "ctxT":
                    pe.wait_ge(ctx_loaded, st.count("proj", 16, 16))
                    last = transposed(ps, ctx_in)
                elif name == "keys":
                    need("ctxT")
                    last = product(ps, weight(2), ctxT)
                elif name == "queries":
                    need("x2T")
                    last = product(ps, weight(1), x2T)
                elif name == "values":
                    last = product(ps, ctxT, weight(3))
                elif name == "selfY":
                    need("xT")
                    last = product(ps, wqk, xT)
                elif name == "selfV":
                    last = product(ps, xT, weight(0))
                elif name == "selfS":
                    need("selfY")
                    last = product(ps, selfY, xT)
                elif name == "selfPT":
                    need("selfS")
                    last = transposed(ps, self_p[:])
                elif name == "selfO":
                    need("selfPT")
                    last = product(ps, self_pT, selfV)
                elif name.startswith("max"):
                    g = int(name[3])
                    stage = STAGE[name]
                    pe.wait_ge(max_found, st.count(stage, H, 4 * g + 4))
                    for t in range(T):
                        last = t_.transpose(ps[0:4, 0, t * P:(t + 1) * P], maxima[:, t, 4 * g:4 * g + 4], ident[:])
                elif name == "logits":
                    need("x3T")
                    last = accumulate(ps[0:2 * E, 0, :], [([w[:, c, :] for w in cwT], [x[:, c, :] for x in x3T])
                                                          for c in range(C)])
                elif name == "logitsT":
                    need("logits")
                    for t in range(T):
                        last = t_.transpose(ps[:, 0, t * P:(t + 1) * P], logits_s[:, t * P:(t + 1) * P], ident[:])
                elif name == "gatesT":
                    pe.wait_ge(gates_ready, st.count("ffn", 1, 1))
                    for t in range(T):
                        last = t_.transpose(ps[0:QROWS, 0, t * P:(t + 1) * P], gates[:, t, :], ident[:])
                elif name.startswith("hidden"):
                    i = int(name[6])
                    if i == 0 and st.round is None and st.s == LAG["ffn"] or st.s == FULL_FROM:
                        pe.wait_ge(experts_split, 4)
                    for k in range(2):
                        last = accumulate(ps[:, k], [([w[:, c, 2 * i + k, :] for w in w1s], [x[:, c, :] for x in x3T])
                                                     for c in range(C)])
                elif name.startswith("gate"):
                    i = int(name[4])
                    if i == 0:
                        need("gatesT")
                    for k in range(2):
                        last = t_.matmul(ps[:, k], onehot[:, 2 * i + k, :], gatesT[:], start=True, stop=True)
                elif name.startswith("natural"):
                    t = int(name[7])
                    pe.wait_ge(att_copied, st.count("late", 2, 2))
                    flat = ps[:].rearrange("p a b -> p (a b)")
                    for g in range(4):
                        last = t_.transpose(flat[:, g * P:(g + 1) * P], att[:, g, t * P:(t + 1) * P], ident[:])
                elif name == "attT":
                    need("natural1")
                    last = transposed(ps, att_n[:])
                elif name == "wo":
                    need("attT")
                    last = product(ps, attT, weight(4))
                elif name == "out":
                    for t in range(T):
                        tokens = slice(t * P, (t + 1) * P)
                        t_.matmul(ps[:, t], gatesT[:, tokens], b2s[:], start=True, stop=False)
                        for e in range(E):
                            if t == 0 and e % 2 == 0:
                                pe.wait_ge(gated_split, st.count("ffn", 4, e // 2 + 1))
                            last = accumulate(ps[:, t], [([g[:, e, tokens] for g in gated], [w[:, e, :] for w in w2s])],
                                              first=False, final=e == E - 1)
                finish(last, name)

            def step(st):
                for h in range(H):
                    if h < 8 and st.has("late"):
                        scoresT(st, "late", h + 8)
                    if h >= 8 and st.has("score"):
                        scoresT(st, "score", h - 8)
                    if st.has("score"):
                        scores(st, h)
                    for slot, name, stage in tables(st.s)[0]:
                        if slot == h and st.has(stage):
                            work(st, name)
                    if h == 15 and st.has("proj"):
                        copied(pe, st, "values")
                    if h <= 8 and st.has("late"):
                        values_product(st, "late", h + 7)
                    if h >= 9 and st.has("score"):
                        values_product(st, "score", h - 9)

            run(pe, step)


_INS = ["x", "ctx_1024", "mask_1x1xSxS2_ik0", "L0_attn_Wq", "L0_attn_Wk", "L0_attn_Wv", "L0_xattn_wq", "L0_xattn_wk",
        "L0_xattn_wv", "L0_xattn_wo", "L0_ffn_w1", "L0_ffn_b1", "L0_ffn_w2", "L0_ffn_b2", "L0_ffn_centroids",
        "L0_ffn_w_route"]


def shape_constants():
    import numpy as np
    ident = np.eye(P, dtype=np.float32)
    onehot = np.zeros((QROWS, E, P), np.float32)
    for e in range(E):
        onehot[e, e] = 1.0
        onehot[32 + e, e] = 1.0
    inv_freq = (np.float32(1.0) / np.float32(10000.0) ** (np.arange(0, DK, 2, dtype=np.float32) / np.float32(DK)))
    angle = np.arange(S, dtype=np.float32)[None, :] * np.concatenate([inv_freq, inv_freq])[:, None].astype(np.float32)
    sign = np.where(np.arange(DK) % 2 == 0, -1.0, 1.0).astype(np.float32)[:, None]
    cos = np.tile(np.cos(angle).astype(np.float32), (HC, 1))
    sin = np.tile(np.sin(angle).astype(np.float32) * sign, (HC, 1))
    return {"c_ident": ident, "c_onehot": onehot.reshape(QROWS, E * P), "c_cos": cos, "c_sin": sin}


def kernel(**inputs):
    import numpy as np
    import concourse.bacc as bacc
    from concourse import mybir as _mybir
    from concourse.bass_utils import run_bass_kernel_spmd

    nc = bacc.Bacc("TRN2", target_bir_lowering=False, num_devices=1)
    arrays, args = {}, []
    for name in _INS:
        a = np.ascontiguousarray(inputs[name])
        arrays[f"in_{name}"] = a
        args.append(nc.dram_tensor(f"in_{name}", a.shape, _mybir.dt.from_np(a.dtype), kind="ExternalInput").ap())
    for name, a in shape_constants().items():
        arrays[name] = np.ascontiguousarray(a)
        args.append(nc.dram_tensor(name, a.shape, _mybir.dt.from_np(a.dtype), kind="ExternalInput").ap())
    args.append(nc.dram_tensor("out_dram", (B, S, D), F32, kind="ExternalOutput").ap())
    decoder_layer(nc, *args)
    r = run_bass_kernel_spmd(nc, [arrays], core_ids=[0])
    return r.results[0]["out_dram"]
```

```python
from contextlib import ExitStack

import concourse.bass as bass
from concourse import mybir

ALU = mybir.AluOpType
ACT = mybir.ActivationFunctionType
AX_X = mybir.AxisListType.X
F32 = mybir.dt.float32
F32R = mybir.dt.float32r
BF16 = mybir.dt.bfloat16
I32 = mybir.dt.int32

P = 128
B = 16
S = 256
T = S // P
D = 256
C = D // P
H = 16
DK = D // H
HC = P // DK
E = 8
DE = 128
EPS = 1e-5
MASKED = -float(2 ** 32)
INV_SQRT_D = 1.0 / 16.0
INV_SQRT_DK = 0.25
NORM_MAX = 1e12

LAG = {"self": 0, "proj": 1, "score": 2, "late": 3, "ffn": 4}
LAST_LAG = 4
STEPS = B + LAST_LAG
FULL_FROM, FULL_TO = LAST_LAG, B

QROWS = 96
STACKED = 6 * 16
MROWS = 98
VW = 2 * DK
NPROBS = 4
LOWEST = -3.0e38
RING = 8
PARTS = ((0, 1), (1, 2), (2, 4))
SETUP = 11
SMALL_SET = 7
BUFFERS_SET = 4
STACKS_SET = 3
CENTROIDS_MADE = 8

WORK = [
    (0, "max3", "late"), (0, "ctxT", "proj"), (0, "x3T", "ffn"), (1, "x2T", "proj"), (1, "keys", "proj"),
    (2, "logits", "ffn"), (3, "logitsT", "ffn"), (3, "xT", "self"), (3, "queries", "proj"), (5, "max0", "score"),
    (5, "selfY", "self"), (6, "selfV", "self"), (6, "selfS", "self"), (6, "gatesT", "ffn"), (7, "hidden0", "ffn"),
    (7, "gate0", "ffn"), (7, "hidden1", "ffn"), (7, "gate1", "ffn"), (7, "hidden2", "ffn"), (7, "gate2", "ffn"),
    (7, "hidden3", "ffn"), (7, "gate3", "ffn"), (8, "max1", "score"), (8, "selfPT", "self"), (9, "values", "proj"),
    (10, "natural1", "late"), (10, "natural0", "late"), (11, "selfO", "self"), (11, "attT", "late"),
    (11, "max2", "score"), (13, "wo", "late"), (15, "out", "ffn"),
]
HEAD_WORK = [
    (0, "max3", "late"), (0, "ctxT", "proj"), (1, "x2T", "proj"), (2, "keys", "proj"), (3, "queries", "proj"),
    (3, "xT", "self"), (5, "max0", "score"), (5, "selfY", "self"), (6, "selfV", "self"), (6, "selfS", "self"),
    (8, "max1", "score"), (9, "selfPT", "self"), (9, "values", "proj"), (10, "selfO", "self"),
    (10, "natural0", "late"), (10, "natural1", "late"), (12, "attT", "late"), (12, "max2", "score"),
    (13, "wo", "late"),
]
TAIL_WORK = [
    (0, "max3", "late"), (0, "ctxT", "proj"), (1, "x3T", "ffn"), (1, "x2T", "proj"), (2, "keys", "proj"),
    (2, "logits", "ffn"), (3, "logitsT", "ffn"), (4, "queries", "proj"), (6, "max0", "score"), (7, "gatesT", "ffn"),
    (7, "hidden0", "ffn"), (7, "gate0", "ffn"), (7, "hidden1", "ffn"), (7, "gate1", "ffn"), (7, "hidden2", "ffn"),
    (7, "gate2", "ffn"), (7, "hidden3", "ffn"), (7, "gate3", "ffn"), (8, "max1", "score"), (9, "values", "proj"),
    (10, "natural0", "late"), (10, "natural1", "late"), (11, "attT", "late"), (12, "max2", "score"),
    (13, "wo", "late"), (15, "out", "ffn"),
]
NBANKS = 3
BANK = {name: i % NBANKS for i, (_, name, _) in enumerate(WORK)}
STAGE = {name: stage for _, name, stage in WORK}

SPLIT = ("ctxT", "x3T", "x2T", "xT", "selfY", "selfV", "selfPT", "attT")

ACT_WORK = [
    (0, "ctxT", "proj"), (0, "x3T", "ffn"), (1, "attention0", "late"), (1, "x2T", "proj"), (2, "logits", "ffn"),
    (2, "xT", "self"), (2, "round_k", "proj"), (4, "selfY", "self"), (4, "gate_exp", "ffn"), (6, "round_q", "proj"),
    (6, "selfV", "self"), (6, "softmax", "self"), (6, "gatesT", "ffn"), (7, "gelu0", "ffn"), (7, "gelu1", "ffn"),
    (7, "gated0", "ffn"), (7, "gelu2", "ffn"), (7, "gated1", "ffn"), (7, "gelu3", "ffn"), (7, "gated2", "ffn"),
    (8, "attention1", "late"), (8, "gated3", "ffn"), (8, "selfPT", "self"), (9, "values", "proj"),
    (10, "attT", "late"),
]
HEAD_ACT_WORK = [
    (0, "attention0", "late"), (0, "ctxT", "proj"), (1, "x2T", "proj"), (2, "xT", "self"), (3, "round_k", "proj"),
    (4, "selfY", "self"), (5, "selfV", "self"), (7, "round_q", "proj"), (7, "softmax", "self"),
    (7, "attention1", "late"), (9, "selfPT", "self"), (9, "values", "proj"), (11, "attT", "late"),
]
TAIL_ACT_WORK = [
    (0, "attention0", "late"), (0, "ctxT", "proj"), (1, "x3T", "ffn"), (1, "x2T", "proj"), (2, "logits", "ffn"),
    (3, "round_k", "proj"), (4, "gate_exp", "ffn"), (6, "gatesT", "ffn"), (7, "gelu0", "ffn"), (7, "gelu1", "ffn"),
    (7, "gated0", "ffn"), (7, "gelu2", "ffn"), (7, "gated1", "ffn"), (7, "gated2", "ffn"), (7, "gelu3", "ffn"),
    (7, "round_q", "proj"), (8, "attention1", "late"), (8, "gated3", "ffn"), (9, "values", "proj"),
    (10, "attT", "late"),
]

DVE_WORK = [
    (0, "max3", "late"), (0, "ctxT", "proj"), (0, "moments_self", "self"), (0, "x3T", "ffn"), (1, "turn_k", "proj"),
    (1, "x2T", "proj"), (2, "normal_self", "self"), (2, "gate_logits", "ffn"), (3, "xT", "self"),
    (4, "turn_q", "proj"), (5, "max0", "score"), (5, "selfY", "self"), (5, "gate_weights", "ffn"),
    (6, "self_max", "self"), (6, "selfV", "self"), (6, "gates_low", "ffn"), (7, "gate0", "ffn"),
    (7, "gate1", "ffn"), (7, "low0", "ffn"), (7, "gate2", "ffn"), (7, "low1", "ffn"), (7, "gate3", "ffn"),
    (7, "low2", "ffn"), (8, "max1", "score"), (8, "low3", "ffn"), (8, "selfPT", "self"), (10, "natural0", "late"),
    (10, "natural1", "late"), (11, "add_self", "self"), (11, "attT", "late"), (11, "max2", "score"),
    (13, "wo", "late"), (13, "moments_ahead", "any"), (14, "normal_ahead", "any"), (15, "out", "ffn"),
]
HEAD_DVE_WORK = [
    (0, "max3", "late"), (0, "moments_self", "self"), (0, "ctxT", "proj"), (1, "x2T", "proj"),
    (2, "turn_k", "proj"), (2, "normal_self", "self"), (3, "turn_q", "proj"), (3, "xT", "self"),
    (5, "max0", "score"), (5, "selfY", "self"), (6, "selfV", "self"), (6, "self_max", "self"), (8, "max1", "score"),
    (9, "selfPT", "self"), (10, "add_self", "self"), (10, "natural0", "late"), (10, "natural1", "late"),
    (12, "attT", "late"), (12, "max2", "score"), (13, "wo", "late"), (13, "moments_ahead", "any"),
    (15, "normal_ahead", "any"),
]
TAIL_DVE_WORK = [
    (0, "max3", "late"), (0, "ctxT", "proj"), (1, "x3T", "ffn"), (1, "x2T", "proj"), (2, "turn_k", "proj"),
    (2, "gate_logits", "ffn"), (4, "turn_q", "proj"), (5, "gate_weights", "ffn"), (6, "max0", "score"),
    (6, "gates_low", "ffn"), (7, "gate0", "ffn"), (7, "gate1", "ffn"), (7, "low0", "ffn"), (7, "gate2", "ffn"),
    (7, "low1", "ffn"), (7, "gate3", "ffn"), (8, "max1", "score"), (8, "low2", "ffn"), (8, "low3", "ffn"),
    (10, "natural0", "late"), (10, "natural1", "late"), (11, "attT", "late"), (12, "max2", "score"),
    (13, "wo", "late"), (13, "moments_ahead", "any"), (15, "normal_ahead", "any"), (15, "out", "ffn"),
]


def active(s):
    return [g for g in LAG if 0 <= s - LAG[g] < B]


def tables(s):
    if s < FULL_FROM:
        return HEAD_WORK, HEAD_ACT_WORK, HEAD_DVE_WORK
    if s >= FULL_TO:
        return TAIL_WORK, TAIL_ACT_WORK, TAIL_DVE_WORK
    return WORK, ACT_WORK, DVE_WORK


def uses_before(s, name):
    k = BANK[name]
    n = 0
    for step in range(s + 1):
        for _, other, stage in tables(step)[0]:
            if BANK[other] == k and stage in active(step):
                n += 1
            if step == s and other == name:
                return n


class Step:

    def __init__(self, s, round=None):
        self.s, self.round = s, round
        self.stages = active(s)

    def has(self, stage):
        if stage == "any":
            return "self" in self.stages or "late" in self.stages
        return stage in self.stages

    def batch(self, stage):
        b = self.s - LAG[stage]
        return b if self.round is None else self.round * 2 + b

    def parity(self, stage):
        return (self.s - LAG[stage]) % 2

    def number(self, per_step, done):
        n = per_step * self.s + done
        return n if self.round is None else self.round * (2 * per_step) + n

    def count(self, stage, per_batch, done):
        n = per_batch * (self.s - LAG[stage]) + done
        return n if self.round is None else self.round * (2 * per_batch) + n

    def turn(self, name, steps_ago=0):
        s = self.s - steps_ago
        n = uses_before(s, name)
        if self.round is None:
            return n
        return self.round * (uses_before(s + 2, name) - n) + n


LN_COLUMNS = (slice(0, 2), slice(2, 8))
LN_CALLS = (lambda st: lambda per_pass, done: st.count("self", per_pass, done),
            lambda st: st.number)


def wait(engine, semaphore, value):
    if isinstance(value, int) and value <= 0:
        return
    engine.wait_ge(semaphore, value)


def decoder_layer(nc, x, ctx, mask, Wq, Wk, Wv, wq, wk, wv, wo, w1, b1, w2, b2, cent, route,
                  c_ident, c_onehot, c_cos, c_sin, out):
    with ExitStack() as stack:
        def sb(name, shape, dt=F32):
            return stack.enter_context(nc.sbuf_tensor(name, shape, dt))

        def parts(name, shape):
            return sb(name + "_hi", shape, F32R), sb(name + "_lo", shape, F32R)

        def bank(name):
            return stack.enter_context(nc.psum_tensor(name, [P, 2, 256], F32))

        def sem(name):
            return stack.enter_context(nc.semaphore(name))

        scores_ps = [bank("scores0_ps"), bank("scores1_ps")]
        scoresT_ps = [bank("scoresT0_ps"), bank("scoresT1_ps")]
        pv_ps = bank("pv_ps")
        work_ps = [bank(f"work{k}_ps") for k in range(NBANKS)]

        parts_dram = nc.dram_tensor("parts", (2, 2, 2, P, C, S), F32).ap()

        ident = sb("ident", [P, P])
        ident_b = sb("ident_b", [P, P], BF16)
        cos_k = sb("cos_k", [P, S])
        sin_k = sb("sin_k", [P, S])
        cos_q = sb("cos_q", [P, S])
        sin_q = sb("sin_q", [P, S])
        onehot = sb("onehot", [QROWS, E, P], F32R)
        wqk = parts("wqk", [P, C, D])
        wT = parts("wT", [P, 5, C, D])
        w1s = parts("w1s", [P, C, E, DE])
        w2s = parts("w2s", [P, E, D])
        b1T = sb("b1T", [P, E])
        b2s = sb("b2s", [QROWS, D], F32R)
        cwT = parts("cwT", [P, C, 2 * E])
        cst = sb("cst", [E, 8])
        maskN = sb("maskN", [P, T, S])
        maskT = sb("maskT", [P, T, S], BF16)
        alive = sb("alive", [P, T])
        dead = sb("dead", [P, T])
        zero_col = sb("zero_col", [P, 1])
        carrier = sb("carrier", [P, 7])
        half_c = sb("half_c", [P, 8])
        three_c = sb("three_c", [P, 8])
        sixteenth_c = sb("sixteenth_c", [P, T])
        power_c = sb("power_c", [P, 8])

        xr = sb("xr", [P, RING, T, D])
        ctx_in = sb("ctx_in", [P, T, D])

        stats = sb("stats", [P, 6, 6])
        mv = sb("mv", [P, 8, 2])
        rs0 = sb("rs0", [P, 8])
        nw = sb("nw", [P, 4, 8])
        rstd = sb("rstd", [P, 8])
        cosn = sb("cosn", [P, 4, T])
        xT = parts("xT", [P, C, S])
        selfY = parts("selfY", [P, C, S])
        selfV = parts("selfV", [P, T, D])
        self_max = sb("self_max", [P, T])
        self_bias = sb("self_bias", [P, T])
        self_sum = sb("self_sum", [P, T])
        self_rec = sb("self_rec", [P, T])
        self_p = sb("self_p", [P, T, S])
        xn_stream = sb("xn_stream", [P, T, D])
        xn = [xn_stream, xn_stream, self_p]
        self_pT = selfY
        ctxT = parts("ctxT", [P, C, S])
        x2T = parts("x2T", [P, C, S])
        rope_hi = [sb("rope_hi_k", [P, C, S], F32R), sb("rope_hi_q", [P, C, S], F32R)]
        rope_lo = [sb("rope_lo_k", [P, C, S], F32R), sb("rope_lo_q", [P, C, S], F32R)]
        rope_a = [t[:].bitcast(F32) for t in rope_lo]
        rope_b = [sb("rope_b_k", [P, C, S]), sb("rope_b_q", [P, C, S])]
        kstack = sb("kstack", [P, H, S], F32R)
        qstack = sb("qstack", [P, H, S], F32R)
        vals = [sb("vals0", [P, T, H, VW]), sb("vals1", [P, T, H, VW])]
        maxima = sb("maxima", [P, T, H])
        mrow_hi = sb("mrow_hi", [4, 2, S], F32R)
        mrow_lo = sb("mrow_lo", [4, 2, S], F32R)
        probs = sb("probs", [P, NPROBS, T, S])
        att = sb("att", [P, 4, S])
        att_rec = sb("att_rec", [P, T, H])
        att_n = self_p
        attT = x2T
        x3T = parts("x3T", [P, C, S])
        logits_s = sb("logits_s", [P, S])
        logits2 = sb("logits2", [P, T, 2 * E])
        logit = sb("logit", [P, T, E])
        top = sb("top", [P, T, 8])
        shifted = sb("shifted", [P, T, E])
        expd = sb("expd", [P, T, E])
        kept = sb("kept", [P, T, E])
        ksum = sb("ksum", [P, T])
        krec = sb("krec", [P, T])
        gates = sb("gates", [P, T, QROWS])
        gatesT = sb("gatesT", [QROWS, S], F32R)
        hidden = sb("hidden", [P, 4, S])
        gated = parts("gated", [P, E, S])
        raw = ([hidden[:, 2 * i:2 * i + 2] for i in range(2)] + [t[:] for t in rope_b]
               + [probs[:, i] for i in range(3)])
        raw_experts = hidden[:]
        raw_mask = probs[:, 3].bitcast(I32)
        onehot_f = att[0:QROWS]
        raw_b2 = xr[0:QROWS, RING - 1, 0]
        csq = xr[0:E, RING - 2, 0]
        raw_b = xr[0:E, RING - 1, 1, 0:DE]
        raw_r = self_p[0:32 + E, 1]
        alive_b = self_p[:, 0].rearrange("p (t m) -> p t m", t=T)

        consts_loaded = sem("consts_loaded")
        ident_loaded = sem("ident_loaded")
        mask_loaded = sem("mask_loaded")
        weight_loaded = [sem(f"{name}_loaded") for name in ("Wq", "Wk", "Wv", "wq", "wk", "wv", "wo")]
        experts_loaded = sem("experts_loaded")
        small_loaded = sem("small_loaded")
        b2_loaded = sem("b2_loaded")
        x_loaded = [sem(f"x_loaded{i}") for i in range(len(PARTS))]
        x_ahead = [sem("x_ahead_even"), sem("x_ahead_odd")]
        ctx_loaded = sem("ctx_loaded")
        b2_zeroed = sem("b2_zeroed")
        small_set = sem("small_set")
        stacks_set = sem("stacks_set")
        buffers_set = sem("buffers_set")
        constants_made = sem("constants_made")
        cent_square = sem("cent_square")
        cent_newton = sem("cent_newton")
        setup_rounded = sem("setup_rounded")
        experts_rounded = sem("experts_rounded")
        experts_split = sem("experts_split")
        setup_formed = sem("setup_formed")
        setup_copied = sem("setup_copied")
        work_ready = [sem(f"work{k}_ready") for k in range(NBANKS)]
        work_copied = [sem(f"work{k}_copied") for k in range(NBANKS)]
        ln_stats = [sem("ln_stats_self"), sem("ln_stats_ahead")]
        ln_moments = [sem("ln_moments_self"), sem("ln_moments_ahead")]
        ln_var = [sem("ln_var_self"), sem("ln_var_ahead")]
        ln_power = [sem("ln_power_self"), sem("ln_power_ahead")]
        ln_newton = [sem("ln_newton_self"), sem("ln_newton_ahead")]
        xn_ready = [sem("xn_ready_self"), sem("xn_ready_proj"), sem("xn_ready_ffn")]
        cosn_ready = sem("cosn_ready")
        self_max_found = sem("self_max_found")
        self_bias_ready = sem("self_bias_ready")
        self_rec_ready = sem("self_rec_ready")
        rope_mixed = [sem("rope_mixed_k"), sem("rope_mixed_q")]
        rope_summed = [sem("rope_summed_k"), sem("rope_summed_q")]
        rope_rounded = [sem("rope_rounded_k"), sem("rope_rounded_q")]
        rope_split = [sem("rope_split_k"), sem("rope_split_q")]
        parts_saved = [sem("k_parts_saved"), sem("q_parts_saved")]
        stacked = [sem(f"stacked{g}") for g in range(4)]
        scores_ready = sem("scores_ready")
        max_found = sem("max_found")
        mrow_rounded = sem("mrow_rounded")
        mrow_loaded = [sem(f"mrow_loaded{g}") for g in range(4)]
        scoresT_ready = sem("scoresT_ready")
        probs_ready = sem("probs_ready")
        pv_done = sem("pv_done")
        att_copied = sem("att_copied")
        att_rec_ready = sem("att_rec_ready")
        gate_logit = sem("gate_logit")
        gate_top = sem("gate_top")
        gate_shift = sem("gate_shift")
        gate_exp = sem("gate_exp")
        gate_kept = sem("gate_kept")
        gate_rec = sem("gate_rec")
        gates_ready = sem("gates_ready")
        gated_rounded = sem("gated_rounded")
        gated_split = sem("gated_split")
        rounded = {name: sem(f"{name}_rounded") for name in SPLIT}
        gatesT_rounded = sem("gatesT_rounded")
        stored = sem("stored")

        def W(name):
            return work_ps[BANK[name]]

        def begin(pe, st, name):
            wait(pe, work_copied[BANK[name]], st.turn(name) - 1)

        def ready(engine, st, name):
            engine.wait_ge(work_ready[BANK[name]], st.turn(name))

        def copied(engine, st, name, steps_ago=0):
            engine.wait_ge(work_copied[BANK[name]], st.turn(name, steps_ago))

        def setup_parts(i):
            src = setup_banks[i % 4]
            if i == 0:
                return src[:], [t[:] for t in wqk]
            if i <= 5:
                return src[:], [t[:, i - 1] for t in wT]
            pairs = src[:, :, 0:64].rearrange("p c (a e) -> p c a e", a=2)[:, :, :, 0:E]
            return pairs, [t[:].rearrange("p c (a e) -> p c a e", a=2) for t in cwT]

        def experts_part(s, part):
            if s < 2:
                return w1s[part][:, s].rearrange("p e j -> p (e j)")
            return w2s[part][:, 4 * (s - 2):4 * (s - 1)].rearrange("p e d -> p (e d)")

        def rows(t, b):
            return t[:, b] if isinstance(b, int) else t[:, bass.ds(b, 1)].squeeze(1)

        def stream(b):
            return xr[:, b % RING] if isinstance(b, int) else xr[:, bass.ds(b & (RING - 1), 1)].squeeze(1)

        def run(engine, step):
            for s in range(FULL_FROM):
                if s == 1:
                    engine.wait_ge(buffers_set, BUFFERS_SET)
                if s == 2:
                    engine.wait_ge(stacks_set, STACKS_SET)
                step(Step(s))
            with engine.Fori(0, (FULL_TO - FULL_FROM) // 2) as r:
                for u in range(2):
                    step(Step(FULL_FROM + u, r))
            for s in range(FULL_TO, STEPS):
                step(Step(s))

        parts_of = {"ctxT": ctxT, "x3T": x3T, "x2T": x2T, "xT": xT, "selfY": selfY, "selfV": selfV,
                    "selfPT": self_pT, "attT": attT}
        setup_banks = scores_ps + scoresT_ps

        block = stack.enter_context(nc.Block())

        @block.sync
        def _(sp):
            xv = x.rearrange("b (t p) d -> p b t d", p=P)
            cv = ctx.rearrange("b (t p) d -> p b t d", p=P)

            def load(i):
                lo, hi = PARTS[i]
                sp.dma_start(xr[:, lo:hi], xv[:, lo:hi]).then_inc(x_loaded[i], 16)

            sources = (Wq, Wk, Wv, wq, wk, wv, wo)
            for i, w in enumerate(sources[:2]):
                sp.dma_start(raw[i], w.rearrange("(c p) d -> p c d", p=P)).then_inc(weight_loaded[i], 16)
            sp.dma_start(ident[:], c_ident).then_inc(ident_loaded, 16)
            sp.dma_start(raw_mask, mask.rearrange("a b (t p) k -> p (a b t) k", p=P)).then_inc(mask_loaded, 16)
            sp.dma_start(raw[2], Wv.rearrange("(c p) d -> p c d", p=P)).then_inc(weight_loaded[2], 16)
            load(0)
            sp.dma_start(raw_r[0:E], cent).then_inc(small_loaded, 16)
            sp.dma_start(raw_r[32:32 + E], route).then_inc(small_loaded, 16)
            for i in range(3, len(sources)):
                sp.dma_start(raw[i], sources[i].rearrange("(c p) d -> p c d", p=P)).then_inc(weight_loaded[i], 16)
            sp.dma_start(raw_b, b1).then_inc(small_loaded, 16)
            for dst, src in ((cos_k[:], c_cos), (sin_k[:], c_sin),
                             (onehot_f.rearrange("p a b -> p (a b)"), c_onehot)):
                sp.dma_start(dst, src).then_inc(consts_loaded, 16)
            sp.wait_ge(b2_zeroed, 1)
            for i in range(3):
                sp.dma_start(raw_b2[32 * i:32 * i + E], b2).then_inc(b2_loaded, 16)
            for i in range(1, len(PARTS)):
                load(i)
            outv = out.rearrange("b (t p) d -> p b t d", p=P)

            def load_context(st):
                if st.has("proj"):
                    copied(sp, st, "ctxT")
                sp.dma_start(ctx_in[:], rows(cv, st.batch("self"))).then_inc(ctx_loaded, 16)

            def load_experts(s):
                if s == 0:
                    sp.wait_ge(setup_copied, SETUP)
                wait(sp, experts_split, s)
                if s < 2:
                    src = w1[:, s * P:(s + 1) * P, :].rearrange("e p j -> p e j")
                else:
                    src = w2[4 * (s - 2):4 * (s - 1)].rearrange("e j d -> j e d")
                sp.dma_start(raw_experts.rearrange("p a b -> p (a b)").rearrange("p (e j) -> p e j", e=src.shape[1]),
                             src).then_inc(experts_loaded, 16)

            def load_next(st):
                b = st.batch("self") + 1
                source = xv[:, b % B] if isinstance(b, int) else xv[:, bass.ds(b & (B - 1), 1)].squeeze(1)
                sp.dma_start(stream(b), source).then_inc(x_ahead[(st.s + 1) % 2], 16)

            def send_maxima(st, stage, g):
                copied(sp, st, f"max{g}")
                for row, src in ((QROWS, mrow_hi), (QROWS + 1, mrow_lo)):
                    if g == 0 and row > QROWS and st.s >= FULL_FROM and st.has("self"):
                        sp.wait_ge(stored, st.number(16, 1 - 16 * LAST_LAG))
                    sp.dma_start(qstack[row:row + 1, 4 * g:4 * g + 4, :].bitcast(F32),
                                 src[:, g % 2, :].bitcast(F32)).then_inc(mrow_loaded[g], 16)

            def save_parts(st, j):
                if j == 0:
                    wait(sp, stacked[3], st.count("proj", STACKED, -STACKED))
                sp.wait_ge(rope_split[j], st.count("proj", 1, 1))
                for k, src in enumerate((rope_hi[j], rope_lo[j])):
                    if j == 1 and k == 1:
                        sp.wait_ge(parts_saved[0], st.count("proj", 32, 32))
                    sp.dma_start(parts_dram[st.parity("proj"), j, k], src[:].bitcast(F32)).then_inc(parts_saved[j], 16)

            def stack_heads(st, stage, g):
                wait(sp, scoresT_ready, st.count(stage, H, 4 * g + 4 - H))
                c, h0 = 4 * g // HC, 4 * g % HC
                for j, stack_ in enumerate((kstack, qstack)):
                    if g == 0 and j == 1:
                        sp.wait_ge(parts_saved[1], st.count(stage, 32, 32))
                    for r in range(3):
                        part = 1 if r == 1 + j else 0
                        src = parts_dram[st.parity(stage), j, part, DK * h0:DK * (h0 + 4), c]
                        sp.dma_start(stack_[DK * r:DK * r + DK, 4 * g:4 * g + 4, :].bitcast(F32),
                                     src.rearrange("(h d) t -> d h t", d=DK)).then_inc(stacked[g], 16)

            def step(st):
                if st.has("self"):
                    load_context(st)
                if st.round is None and st.s < 4:
                    load_experts(st.s)
                if st.s == 1:
                    sp.wait_ge(stacks_set, STACKS_SET)
                if st.has("late"):
                    send_maxima(st, "late", 3)
                if st.has("score"):
                    stack_heads(st, "score", 2)
                    send_maxima(st, "score", 0)
                if st.has("self") and st.s >= FULL_FROM - 1:
                    load_next(st)
                if st.has("proj"):
                    save_parts(st, 0)
                if st.has("score"):
                    stack_heads(st, "score", 3)
                    send_maxima(st, "score", 1)
                if st.has("proj"):
                    save_parts(st, 1)
                    stack_heads(st, "proj", 0)
                if st.has("score"):
                    send_maxima(st, "score", 2)
                if st.has("proj"):
                    stack_heads(st, "proj", 1)
                if st.has("ffn"):
                    copied(sp, st, "out")
                    b = st.batch("ffn")
                    sp.dma_start(rows(outv, b), stream(b)).then_inc(stored, 16)

            run(sp, step)
            sp.wait_ge(stored, 16 * B + 1)
            sp.wait_ge(x_ahead[0], 16 * ((B - FULL_FROM) // 2 + 1))

        @block.gpsimd
        def _(pool):
            g = nc.gpsimd
            g.memset(raw_b2, 0.0).then_inc(b2_zeroed, 1)
            g.memset(carrier[:, 6:7], 0.0).then_inc(stored, 1)
            for t, value in ((half_c, 0.5), (three_c, 3.0), (sixteenth_c, 1.0 / 16.0), (power_c, -0.5), (mv, 1.0),
                             (gates, 0.0), (logits_s, 0.0)):
                g.memset(t[:], value).then_inc(small_set, 1)
            pool.wait_ge(small_set, SMALL_SET)

            pool.wait_ge(cent_square, 2)
            g.tensor_tensor(cst[:, 2:3], cst[:, 0:1], power_c[0:E, 0:1], ALU.pow).then_inc(cent_newton, 1)
            pool.wait_ge(cent_newton, 1)
            g.tensor_tensor(cst[:, 3:4], cst[:, 2:3], cst[:, 2:3], ALU.mult).then_inc(cent_newton, 1)
            pool.wait_ge(cent_newton, 2)
            g.tensor_tensor(cst[:, 4:5], cst[:, 3:4], cst[:, 0:1], ALU.mult).then_inc(cent_newton, 1)
            pool.wait_ge(cent_newton, 3)
            g.tensor_scalar(cst[:, 5:6], cst[:, 4:5], -0.5, 1.5, ALU.mult, ALU.add).then_inc(cent_newton, 1)
            pool.wait_ge(cent_newton, 4)
            g.tensor_tensor(cst[:, 6:7], cst[:, 5:6], cst[:, 2:3], ALU.mult).then_inc(cent_newton, 1)

            def newton(st, group):
                k = LN_COLUMNS[group]
                n = LN_CALLS[group](st)
                pool.wait_ge(ln_var[group], n(1, 1))
                g.tensor_tensor(rs0[:, k], mv[:, k, 1], power_c[:, k], ALU.pow).then_inc(ln_power[group], 1)
                pool.wait_ge(ln_power[group], n(1, 1))
                g.tensor_tensor(nw[:, 0, k], rs0[:, k], rs0[:, k], ALU.mult)
                g.tensor_tensor(nw[:, 3, k], rs0[:, k], half_c[:, k], ALU.mult).then_inc(ln_newton[group], 1)
                pool.wait_ge(ln_newton[group], n(4, 1))
                g.tensor_tensor(nw[:, 1, k], nw[:, 0, k], mv[:, k, 1], ALU.mult).then_inc(ln_newton[group], 1)
                pool.wait_ge(ln_newton[group], n(4, 2))
                g.tensor_tensor(nw[:, 2, k], three_c[:, k], nw[:, 1, k], ALU.subtract).then_inc(ln_newton[group], 1)
                pool.wait_ge(ln_newton[group], n(4, 3))
                g.tensor_tensor(rstd[:, k], nw[:, 2, k], nw[:, 3, k], ALU.mult).then_inc(ln_newton[group], 1)

            def inverse_norm(st):
                pool.wait_ge(ln_newton[1], st.number(4, 4))
                g.tensor_tensor(cosn[:, 0], rstd[:, 6:8], rstd[:, 4:6], ALU.mult).then_inc(cosn_ready, 1)
                pool.wait_ge(cosn_ready, st.count("late", 3, 1))
                g.tensor_tensor(cosn[:, 1], cosn[:, 0], mv[:, 4:6, 1], ALU.mult).then_inc(cosn_ready, 1)
                pool.wait_ge(cosn_ready, st.count("late", 3, 2))
                g.tensor_tensor(cosn[:, 2], cosn[:, 1], sixteenth_c[:], ALU.mult).then_inc(cosn_ready, 1)

            def rope(st, j):
                sin = (sin_k, sin_q)[j]
                copied(pool, st, ("keys", "queries")[j])
                g.tensor_tensor(rope_b[j][:], rope_b[j][:], sin[:].unsqueeze(1).to_broadcast([P, C, S]),
                                ALU.mult).then_inc(rope_mixed[j], 1)
                pool.wait_ge(rope_mixed[j], st.count("proj", 1, 1))
                g.tensor_tensor(rope_a[j], rope_a[j], rope_b[j][:], ALU.add).then_inc(rope_summed[j], 1)
                pool.wait_ge(rope_rounded[j], st.count("proj", 1, 1))
                g.tensor_tensor(rope_lo[j][:], rope_a[j], rope_hi[j][:].bitcast(F32),
                                ALU.subtract).then_inc(rope_split[j], 1)

            def split_experts(s):
                pool.wait_ge(experts_rounded, s + 1)
                g.tensor_tensor(experts_part(s, 1), raw_experts.rearrange("p a b -> p (a b)"),
                                experts_part(s, 0).bitcast(F32), ALU.subtract).then_inc(experts_split, 1)

            def step(st):
                if st.has("self"):
                    newton(st, 0)
                if st.s == 0 and st.round is None:
                    for i in range(2):
                        g.memset(vals[i][:], 1.0).then_inc(buffers_set, 1)
                    g.memset(qstack[:].bitcast(F32), 0.0).then_inc(stacks_set, 1)
                    g.memset(kstack[:].bitcast(F32), 0.0).then_inc(stacks_set, 1)
                if st.has("proj"):
                    rope(st, 0)
                    rope(st, 1)
                if st.has("self") or st.has("late"):
                    newton(st, 1)
                if st.has("late"):
                    inverse_norm(st)
                if st.round is None and st.s < 4:
                    split_experts(st.s)
                if st.s == 0:
                    pool.wait_ge(stacks_set, 2)
                    pool.wait_ge(experts_split, 1)
                    g.memset(kstack[QROWS:MROWS].bitcast(F32), -1.0).then_inc(stacks_set, 1)
                    pool.wait_ge(stacks_set, 3)

            run(pool, step)

        @block.scalar
        def _(act):
            a = nc.scalar
            a.preload_act_table(ACT.Exp)
            for i in range(7):
                act.wait_ge(setup_formed, i + 1)
                src, (hi, lo) = setup_parts(i)
                a.copy(hi, src).then_inc(setup_rounded, 1)
            act.wait_ge(consts_loaded, 48)
            a.copy(onehot[:], onehot_f.rearrange("p a b -> p (a b)").rearrange("p (e j) -> p e j", e=E)).then_inc(
                buffers_set, 1)

            def copy_out(st, name, dst, src=None):
                ready(act, st, name)
                a.copy(dst, W(name)[:] if src is None else src).then_inc(work_copied[BANK[name]], 1)

            def round_out(st, name):
                ready(act, st, name)
                a.copy(parts_of[name][0][:], W(name)[:]).then_inc(rounded[name], 1)

            def round_experts(s):
                act.wait_ge(experts_loaded, 16 * (s + 1))
                a.copy(experts_part(s, 0), raw_experts.rearrange("p a b -> p (a b)")).then_inc(experts_rounded, 1)

            def round_gated(st, i):
                copied(act, st, f"gate{i}")
                k = 2 * i % 4
                a.copy(gated[0][:, 2 * i:2 * i + 2], hidden[:, k:k + 2]).then_inc(gated_rounded, 1)

            def softmax(st, stage, h):
                act.wait_ge(scoresT_ready, st.count(stage, H, h + 1))
                wait(act, pv_done, st.count(stage, H, h + 1 - NPROBS))
                a.activation(probs[:, h % NPROBS], scoresT_ps[h % 2][:], ACT.Exp, bias=zero_col[:],
                             scale=INV_SQRT_DK).then_inc(probs_ready, 1)

            def copy_attention(st, half):
                act.wait_ge(pv_done, st.count("late", H, 8 * half + 8))
                a.copy(att[:, 2 * half:2 * half + 2, :], pv_ps[:]).then_inc(att_copied, 1)

            def rope_round(st, j):
                act.wait_ge(rope_summed[j], st.count("proj", 1, 1))
                a.copy(rope_hi[j][:], rope_a[j]).then_inc(rope_rounded[j], 1)

            def expert_rows(st, i):
                name = f"hidden{i}"
                if i >= 2:
                    act.wait_ge(gated_split, st.count("ffn", 4, i - 1))
                ready(act, st, name)
                for k in range(2):
                    e = 2 * i + k
                    last = a.activation(hidden[:, e % 4], W(name)[:, k], ACT.Gelu, bias=b1T[:, e:e + 1])
                last.then_inc(work_copied[BANK[name]], 1)

            def gate_exponentials(st):
                act.wait_ge(gate_shift, st.count("ffn", 1, 1))
                a.activation(expd[:], shifted[:], ACT.Exp, bias=zero_col[:]).then_inc(gate_exp, 1)

            def gates_out(st):
                ready(act, st, "gatesT")
                a.copy(gatesT[:], W("gatesT")[0:QROWS, 0, :]).then_inc(gatesT_rounded, 1)

            def self_softmax(st):
                act.wait_ge(self_bias_ready, st.count("self", 1, 1))
                for t in range(T):
                    last = a.activation(self_p[:, t], W("selfS")[:, t], ACT.Exp, bias=self_bias[:, t:t + 1],
                                        scale=INV_SQRT_D, accum_out=self_sum[:, t:t + 1])
                last.then_inc(work_copied[BANK["selfS"]], 1)

            actions = {
                "attention0": lambda st: copy_attention(st, 0),
                "attention1": lambda st: copy_attention(st, 1),
                "logits": lambda st: copy_out(st, "logits", logits_s[0:2 * E, :], W("logits")[0:2 * E, 0, :]),
                "round_k": lambda st: rope_round(st, 0),
                "round_q": lambda st: rope_round(st, 1),
                "gate_exp": gate_exponentials,
                "softmax": self_softmax,
                "gatesT": gates_out,
                "gelu0": lambda st: expert_rows(st, 0),
                "gelu1": lambda st: expert_rows(st, 1),
                "gelu2": lambda st: expert_rows(st, 2),
                "gelu3": lambda st: expert_rows(st, 3),
                "values": lambda st: copy_out(st, "values", vals[st.parity("proj")][:, :, :, 0:DK],
                                              W("values")[:].rearrange("p t (h d) -> p t h d", h=H)),
                "gated0": lambda st: round_gated(st, 0),
                "gated1": lambda st: round_gated(st, 1),
                "gated2": lambda st: round_gated(st, 2),
                "gated3": lambda st: round_gated(st, 3),
            }

            def step(st):
                for h in range(H):
                    if h < 8 and st.has("late"):
                        softmax(st, "late", h + 8)
                    if h >= 8 and st.has("score"):
                        softmax(st, "score", h - 8)
                    for slot, name, stage in tables(st.s)[1]:
                        if slot == h and st.has(stage):
                            if name in SPLIT:
                                round_out(st, name)
                            else:
                                actions[name](st)
                if st.round is None and st.s < 4:
                    round_experts(st.s)

            run(act, step)

        @block.vector
        def _(dve):
            v = nc.vector
            made = [0]

            def chain(ins):
                made[0] += 1
                ins.then_inc(constants_made, 1)
                dve.wait_ge(constants_made, made[0])

            def carry(i):
                v.memset(carrier[:, i:i + 1], 0.0)

            def moments(st, group):
                n = LN_CALLS[group](st)
                if group == 0:
                    for i, (lo, hi) in enumerate(PARTS):
                        if st.s == lo:
                            dve.wait_ge(x_loaded[i], 16)
                    if st.round is not None:
                        dve.wait_ge(x_ahead[st.s % 2], st.round * 16 + 16)
                    parts = [(0, "self")]
                else:
                    parts = [(1, "self")] * st.has("self") + [(2, "late")] * st.has("late")
                    carry(5)
                for i, stage in parts:
                    x_rows = stream(st.batch(stage))
                    for t in range(T):
                        last = v.bn_stats(stats[:, 2 * i + t], x_rows[:, t])
                last.then_inc(ln_stats[group], 1)
                dve.wait_ge(ln_stats[group], n(1, 1))
                carry(2 if group else 4)
                for i, _ in parts:
                    for t in range(T):
                        last = v.bn_aggr(mv[:, 2 * i + t], stats[:, 2 * i + t])
                last.then_inc(ln_moments[group], 1)
                dve.wait_ge(ln_moments[group], n(1 + group, 1))
                if group == 1:
                    v.tensor_scalar(mv[:, 6:8, 1], mv[:, 4:6, 1], 1e-37, None, ALU.max).then_inc(ln_moments[group], 1)
                    dve.wait_ge(ln_moments[group], n(2, 2))
                k = slice(0, 2) if group == 0 else slice(2, 6)
                v.tensor_scalar(mv[:, k, 1], mv[:, k, 1], EPS, None, ALU.add).then_inc(ln_var[group], 1)

            def normalise(st, group, i, stage):
                dve.wait_ge(ln_newton[group], LN_CALLS[group](st)(4, 4))
                x_rows = stream(st.batch(stage))
                for t in range(T):
                    k = 2 * i + t
                    last = v.tensor_scalar(xn[i][:, t], x_rows[:, t], mv[:, k, 0:1], rstd[:, k:k + 1],
                                           ALU.subtract, ALU.mult)
                last.then_inc(xn_ready[i], 1)

            chain(v.memset(zero_col[:], 0.0))
            dve.wait_ge(ident_loaded, 16)
            v.tensor_copy(ident_b[:], ident[:]).then_inc(setup_copied, 1)
            dve.wait_ge(mask_loaded, 16)
            chain(v.tensor_scalar(maskN[:], raw_mask, 0.0, None, ALU.not_equal))
            chain(v.tensor_reduce(alive[:], maskN[:], AX_X, ALU.max))
            chain(v.tensor_scalar(dead[:], alive[:], -1.0, 1.0, ALU.mult, ALU.add))
            for t in range(T):
                v.tensor_scalar(alive_b[:, t], ident[:], 0.0, alive[:, t:t + 1], ALU.mult, ALU.add)
                chain(v.tensor_scalar(maskN[:, t], maskN[:, t], dead[:, t:t + 1], 1.0, ALU.max, ALU.subtract))
            chain(v.tensor_scalar(maskN[:], maskN[:], -MASKED, None, ALU.mult))
            for i in range(SETUP - 1):
                if i == 1:
                    dve.wait_ge(small_loaded, 48)
                    v.tensor_tensor_reduce(csq, raw_r[0:E], raw_r[0:E], 1.0, 0.0, ALU.mult, ALU.add,
                                           cst[:, 7:8]).then_inc(cent_square, 1)
                    dve.wait_ge(cent_square, 1)
                    v.tensor_scalar(cst[:, 0:1], cst[:, 7:8], 1e-24, None, ALU.max).then_inc(cent_square, 1)
                if i == 2:
                    dve.wait_ge(small_set, SMALL_SET)
                    moments(Step(0), 0)
                if i == 3:
                    dve.wait_ge(cent_newton, 5)
                    chain(v.tensor_scalar(raw_r[0:E], raw_r[0:E], cst[:, 6:7], None, ALU.mult))
                dve.wait_ge(setup_formed, i + 1)
                src = setup_banks[i % 4]
                if i <= 6:
                    dve.wait_ge(setup_rounded, i + 1)
                    src, (hi, lo) = setup_parts(i)
                    ins = v.tensor_tensor(lo, src, hi.bitcast(F32), ALU.subtract)
                elif i == 7:
                    ins = v.tensor_copy(b1T[:], src[:, 0, 0:E])
                elif i == 8:
                    dve.wait_ge(consts_loaded, 48)
                    v.tensor_tensor(cos_q[:], cos_k[:], src[:, 0, :], ALU.mult)
                    ins = v.tensor_tensor(sin_q[:], sin_k[:], src[:, 0, :], ALU.mult)
                else:
                    ins = v.tensor_copy(maskT[:], src[:])
                ins.then_inc(setup_copied, 1)
                if i == 5:
                    normalise(Step(0), 0, 0, "self")
            def split_out(st, name):
                dve.wait_ge(rounded[name], st.count(STAGE[name], 1, 1))
                hi, lo = parts_of[name]
                v.tensor_tensor(lo[:], W(name)[:], hi[:].bitcast(F32), ALU.subtract).then_inc(
                    work_copied[BANK[name]], 1)

            def head_max(st, h):
                dve.wait_ge(scores_ready, st.count("score", H, h + 1))
                carry(h % 2)
                for t in range(T):
                    s_ps = scores_ps[h % 2][:, t]
                    last = v.tensor_tensor_reduce(s_ps, s_ps, maskN[:, t], 1.0, LOWEST, ALU.add, ALU.max,
                                                  maxima[:, t, h:h + 1])
                last.then_inc(max_found, 1)

            def round_maxima(st, stage, g):
                name = f"max{g}"
                ready(dve, st, name)
                wait(dve, mrow_loaded[(g + 2) % 4], st.count(stage, 32, 32 if g >= 2 else 0))
                v.tensor_copy(mrow_hi[:, g % 2], W(name)[0:4, 0, :]).then_inc(mrow_rounded, 1)
                dve.wait_ge(mrow_rounded, st.count(stage, 4, g + 1))
                v.tensor_tensor(mrow_lo[:, g % 2], W(name)[0:4, 0, :], mrow_hi[:, g % 2].bitcast(F32),
                                ALU.subtract).then_inc(work_copied[BANK[name]], 1)

            def turn_pairs(st, j):
                name = ("keys", "queries")[j]
                ready(dve, st, name)
                cos = (cos_k, cos_q)[j]
                wait(dve, parts_saved[j], st.count("proj", 32, 0))
                v.tensor_tensor(rope_a[j], W(name)[:], cos[:].unsqueeze(1).to_broadcast([P, C, S]), ALU.mult)
                v.stream_shuffle(rope_b[j][:], W(name)[:], [i ^ 1 for i in range(32)]).then_inc(
                    work_copied[BANK[name]], 1)

            def self_maximum(st):
                ready(dve, st, "selfS")
                v.tensor_reduce(self_max[:], W("selfS")[:], AX_X, ALU.max).then_inc(self_max_found, 1)
                dve.wait_ge(self_max_found, st.count("self", 1, 1))
                v.tensor_scalar(self_bias[:], self_max[:], -INV_SQRT_D, None, ALU.mult).then_inc(self_bias_ready, 1)

            def add_self_attention(st):
                copied(dve, st, "selfS")
                v.reciprocal(self_rec[:], self_sum[:]).then_inc(self_rec_ready, 1)
                dve.wait_ge(self_rec_ready, st.count("self", 1, 1))
                ready(dve, st, "selfO")
                x_rows = stream(st.batch("self"))
                for t in range(T):
                    last = v.scalar_tensor_tensor(x_rows[:, t], W("selfO")[:, t], self_rec[:, t:t + 1], x_rows[:, t],
                                                  ALU.mult, ALU.add)
                last.then_inc(work_copied[BANK["selfO"]], 1)

            def add_to_stream(st, name, stage):
                ready(dve, st, name)
                x_rows = stream(st.batch(stage))
                v.tensor_tensor(x_rows, x_rows, W(name)[:], ALU.add).then_inc(work_copied[BANK[name]], 1)

            def normalise_attention(st, t):
                name = f"natural{t}"
                ready(dve, st, name)
                heads = W(name)[:].rearrange("p a (g w) -> p (a g) w", w=VW)
                v.reciprocal(att_rec[:, t], heads[:, :, DK]).then_inc(att_rec_ready, 1)
                dve.wait_ge(att_rec_ready, st.count("late", T, t + 1))
                v.tensor_tensor(att_n[:, t].rearrange("p (h d) -> p h d", h=H), heads[:, :, 0:DK],
                                att_rec[:, t].unsqueeze(2).to_broadcast([P, H, DK]), ALU.mult).then_inc(
                                    work_copied[BANK[name]], 1)

            def gate_logits(st):
                dve.wait_ge(cosn_ready, st.count("ffn", 3, 3))
                ready(dve, st, "logitsT")
                v.tensor_scalar(cosn[:, 3], cosn[:, 2], NORM_MAX, None, ALU.min)
                v.tensor_copy(logits2[:], W("logitsT")[:, 0].rearrange("p (t e) -> p t e", t=T)[:, :, 0:2 * E]).then_inc(
                    work_copied[BANK["logitsT"]], 1)
                copied(dve, st, "logitsT")
                for t in range(T):
                    last = v.scalar_tensor_tensor(logit[:, t], logits2[:, t, 0:E], cosn[:, 3, t:t + 1],
                                                  logits2[:, t, E:2 * E], ALU.mult, ALU.add)
                last.then_inc(gate_logit, 1)
                dve.wait_ge(gate_logit, st.count("ffn", 1, 1))
                carry(3)
                for t in range(T):
                    last = v.max(top[:, t], logit[:, t])
                last.then_inc(gate_top, 1)
                dve.wait_ge(gate_top, st.count("ffn", 1, 1))
                for t in range(T):
                    last = v.tensor_scalar(shifted[:, t], logit[:, t], top[:, t, 0:1], None, ALU.subtract)
                last.then_inc(gate_shift, 1)

            def gate_weights(st):
                dve.wait_ge(gate_exp, st.count("ffn", 1, 1))
                for t in range(T):
                    last = v.scalar_tensor_tensor(kept[:, t], logit[:, t], top[:, t, 1:2], expd[:, t],
                                                  ALU.is_ge, ALU.mult, accum_out=ksum[:, t:t + 1])
                last.then_inc(gate_kept, 1)
                dve.wait_ge(gate_kept, st.count("ffn", 1, 1))
                v.reciprocal(krec[:], ksum[:]).then_inc(gate_rec, 1)
                dve.wait_ge(gate_rec, st.count("ffn", 1, 1))
                for t in range(T):
                    last = v.tensor_scalar(gates[:, t].rearrange("p (r c) -> p r c", r=3)[:, :, 0:E],
                                           kept[:, t].unsqueeze(1).to_broadcast([P, 3, E]),
                                           krec[:, t:t + 1], None, ALU.mult)
                last.then_inc(gates_ready, 1)

            def gates_low_part(st):
                dve.wait_ge(gatesT_rounded, st.count("ffn", 1, 1))
                v.tensor_tensor(gatesT[32:32 + E], W("gatesT")[32:32 + E, 0, :], gatesT[32:32 + E].bitcast(F32),
                                ALU.subtract).then_inc(work_copied[BANK["gatesT"]], 1)

            def apply_gate(st, i):
                name = f"gate{i}"
                copied(dve, st, f"hidden{i}")
                ready(dve, st, name)
                k = 2 * i % 4
                v.tensor_tensor(hidden[:, k:k + 2], hidden[:, k:k + 2], W(name)[:], ALU.mult).then_inc(
                    work_copied[BANK[name]], 1)

            def low_gated(st, i):
                dve.wait_ge(gated_rounded, st.count("ffn", 4, i + 1))
                k, held = slice(2 * i, 2 * i + 2), slice(2 * i % 4, 2 * i % 4 + 2)
                v.tensor_tensor(gated[1][:, k], hidden[:, held], gated[0][:, k].bitcast(F32),
                                ALU.subtract).then_inc(gated_split, 1)

            def moments_ahead(st):
                if st.has("self"):
                    copied(dve, st, "selfO")
                if st.has("late"):
                    copied(dve, st, "wo")
                moments(st, 1)

            def normalise_ahead(st):
                if st.has("late"):
                    normalise(st, 1, 2, "late")
                if st.has("self"):
                    normalise(st, 1, 1, "self")

            actions = {
                "max3": lambda st: round_maxima(st, "late", 3),
                "max0": lambda st: round_maxima(st, "score", 0),
                "max1": lambda st: round_maxima(st, "score", 1),
                "max2": lambda st: round_maxima(st, "score", 2),
                "moments_self": lambda st: st.s > 0 and moments(st, 0),
                "normal_self": lambda st: st.s > 0 and normalise(st, 0, 0, "self"),
                "turn_k": lambda st: turn_pairs(st, 0),
                "turn_q": lambda st: turn_pairs(st, 1),
                "gate_logits": gate_logits,
                "gate_weights": gate_weights,
                "self_max": self_maximum,
                "gates_low": gates_low_part,
                "gate0": lambda st: apply_gate(st, 0),
                "gate1": lambda st: apply_gate(st, 1),
                "gate2": lambda st: apply_gate(st, 2),
                "gate3": lambda st: apply_gate(st, 3),
                "low0": lambda st: low_gated(st, 0),
                "low1": lambda st: low_gated(st, 1),
                "low2": lambda st: low_gated(st, 2),
                "low3": lambda st: low_gated(st, 3),
                "natural0": lambda st: normalise_attention(st, 0),
                "natural1": lambda st: normalise_attention(st, 1),
                "add_self": add_self_attention,
                "wo": lambda st: add_to_stream(st, "wo", "late"),
                "out": lambda st: add_to_stream(st, "out", "ffn"),
                "moments_ahead": moments_ahead,
                "normal_ahead": normalise_ahead,
            }

            def split_b2():
                dve.wait_ge(b2_loaded, 48)
                chain(v.tensor_copy(b2s[:], raw_b2))
                v.tensor_tensor(b2s[64:QROWS], raw_b2[64:QROWS], b2s[64:QROWS].bitcast(F32), ALU.subtract).then_inc(
                    buffers_set, 1)

            def step(st):
                for h in range(H):
                    if st.s == 0 and h == 5:
                        split_b2()
                    if st.has("score"):
                        head_max(st, h)
                    for slot, name, stage in tables(st.s)[2]:
                        if slot == h and st.has(stage):
                            if name in SPLIT:
                                split_out(st, name)
                            else:
                                actions[name](st)

            run(dve, step)

        @block.tensor
        def _(pe):
            t_ = nc.tensor

            def transposed(dst, src, fill=None):
                for c in range(C):
                    for t in range(T):
                        last = t_.transpose(dst[:, c, t * P:(t + 1) * P], src[:, t, c * P:(c + 1) * P], ident[:])
                return last

            def accumulate(dst, factors, first=True, final=True):
                terms = []
                for left, right in factors:
                    if len(left) == 1:
                        terms.append((left[0], right[0]))
                    else:
                        terms += [(left[0], right[0]), (left[0], right[1]), (left[1], right[0])]
                for i, (left, right) in enumerate(terms):
                    last = t_.matmul(dst, left, right, start=first and i == 0,
                                     stop=final and i == len(terms) - 1)
                return last

            def product(dst, left, right):
                for m in range(2):
                    last = accumulate(dst[:, m], [([l[:, c, m * P:(m + 1) * P] for l in left],
                                                   [r[:, c, :] for r in right]) for c in range(C)])
                return last

            def weight(i):
                return [t[:, i] for t in wT]

            pe.wait_ge(weight_loaded[0], 16)
            pe.wait_ge(weight_loaded[1], 16)
            for i in range(SETUP - 1):
                wait(pe, setup_copied, i - 3 + 1 if i > 3 else 0)
                dst = setup_banks[i % 4]
                if i == 0:
                    last = product(dst, [raw[0]], [raw[1]])
                elif i <= 5:
                    if i == 1:
                        pe.wait_ge(ident_loaded, 16)
                    pe.wait_ge(weight_loaded[1 + i], 16)
                    last = transposed(dst, raw[1 + i])
                elif i == 6:
                    pe.wait_ge(small_loaded, 48)
                    pe.wait_ge(constants_made, CENTROIDS_MADE)
                    for c in range(C):
                        last = t_.transpose(dst[:, c, 0:32 + E], raw_r[0:32 + E, c * P:(c + 1) * P],
                                            ident[0:32 + E, 0:32 + E])
                elif i == 7:
                    last = t_.transpose(dst[:, 0, 0:E], raw_b, ident[0:E, 0:E])
                elif i == 8:
                    for t in range(T):
                        last = t_.matmul(dst[:, 0, t * P:(t + 1) * P], alive_b[:, t], ident[:], start=True, stop=True)
                else:
                    last = transposed(dst, maskN[:])
                last.then_inc(setup_formed, 1)
            pe.wait_ge(setup_copied, SETUP)

            def finish(last, name):
                last.then_inc(work_ready[BANK[name]], 1)

            def scores(st, h):
                if h % 4 == 0:
                    pe.wait_ge(stacked[h // 4], st.count("score", STACKED, STACKED))
                wait(pe, max_found, st.count("score", H, h - 1))
                for t in range(T):
                    last = t_.matmul(scores_ps[h % 2][:, t], qstack[0:QROWS, h, t * P:(t + 1) * P],
                                     kstack[0:QROWS, h, :], start=True, stop=True)
                last.then_inc(scores_ready, 1)

            def scoresT(st, stage, h):
                if h % 4 == 0:
                    pe.wait_ge(mrow_loaded[h // 4], st.count(stage, 32, 32))
                wait(pe, probs_ready, st.count(stage, H, h - 1))
                for t in range(T):
                    t_.matmul(scoresT_ps[h % 2][:, t], kstack[0:MROWS, h, t * P:(t + 1) * P],
                              qstack[0:MROWS, h, :], start=True, stop=False)
                    last = t_.matmul(scoresT_ps[h % 2][:, t], ident_b[:], maskT[:, t], start=False, stop=True)
                last.then_inc(scoresT_ready, 1)

            def values_product(st, stage, h):
                par = st.parity(stage)
                pe.wait_ge(probs_ready, st.count(stage, H, h + 1))
                if h % 8 == 0:
                    wait(pe, att_copied, st.count(stage, 2, h // 8))
                j = h % 4
                for t in range(T):
                    last = t_.matmul(pv_ps[VW * j:VW * j + VW, h // 4 % 2], vals[par][:, t, h, :],
                                     probs[:, h % NPROBS, t], start=t == 0, stop=t == T - 1)
                last.then_inc(pv_done, 1)

            def work(st, name):
                begin(pe, st, name)
                ps = W(name)

                def need(other):
                    if BANK[other] != BANK[name]:
                        copied(pe, st, other)

                if name in ("xT", "x2T", "x3T"):
                    i = ("xT", "x2T", "x3T").index(name)
                    pe.wait_ge(xn_ready[i], st.count(STAGE[name], 1, 1))
                    last = transposed(ps, xn[i])
                elif name == "ctxT":
                    pe.wait_ge(ctx_loaded, st.count("proj", 16, 16))
                    last = transposed(ps, ctx_in)
                elif name == "keys":
                    need("ctxT")
                    last = product(ps, weight(2), ctxT)
                elif name == "queries":
                    need("x2T")
                    last = product(ps, weight(1), x2T)
                elif name == "values":
                    last = product(ps, ctxT, weight(3))
                elif name == "selfY":
                    need("xT")
                    last = product(ps, wqk, xT)
                elif name == "selfV":
                    last = product(ps, xT, weight(0))
                elif name == "selfS":
                    need("selfY")
                    last = product(ps, selfY, xT)
                elif name == "selfPT":
                    need("selfS")
                    last = transposed(ps, self_p[:])
                elif name == "selfO":
                    need("selfPT")
                    last = product(ps, self_pT, selfV)
                elif name.startswith("max"):
                    g = int(name[3])
                    stage = STAGE[name]
                    pe.wait_ge(max_found, st.count(stage, H, 4 * g + 4))
                    for t in range(T):
                        last = t_.transpose(ps[0:4, 0, t * P:(t + 1) * P], maxima[:, t, 4 * g:4 * g + 4], ident[:])
                elif name == "logits":
                    need("x3T")
                    last = accumulate(ps[0:2 * E, 0, :], [([w[:, c, :] for w in cwT], [x[:, c, :] for x in x3T])
                                                          for c in range(C)])
                elif name == "logitsT":
                    need("logits")
                    for t in range(T):
                        last = t_.transpose(ps[:, 0, t * P:(t + 1) * P], logits_s[:, t * P:(t + 1) * P], ident[:])
                elif name == "gatesT":
                    pe.wait_ge(gates_ready, st.count("ffn", 1, 1))
                    for t in range(T):
                        last = t_.transpose(ps[0:QROWS, 0, t * P:(t + 1) * P], gates[:, t, :], ident[:])
                elif name.startswith("hidden"):
                    i = int(name[6])
                    if i == 0 and st.round is None and st.s == LAG["ffn"] or st.s == FULL_FROM:
                        pe.wait_ge(experts_split, 4)
                    for k in range(2):
                        last = accumulate(ps[:, k], [([w[:, c, 2 * i + k, :] for w in w1s], [x[:, c, :] for x in x3T])
                                                     for c in range(C)])
                elif name.startswith("gate"):
                    i = int(name[4])
                    if i == 0:
                        need("gatesT")
                    for k in range(2):
                        last = t_.matmul(ps[:, k], onehot[:, 2 * i + k, :], gatesT[:], start=True, stop=True)
                elif name.startswith("natural"):
                    t = int(name[7])
                    pe.wait_ge(att_copied, st.count("late", 2, 2))
                    flat = ps[:].rearrange("p a b -> p (a b)")
                    for g in range(4):
                        last = t_.transpose(flat[:, g * P:(g + 1) * P], att[:, g, t * P:(t + 1) * P], ident[:])
                elif name == "attT":
                    need("natural1")
                    last = transposed(ps, att_n[:])
                elif name == "wo":
                    need("attT")
                    last = product(ps, attT, weight(4))
                elif name == "out":
                    for t in range(T):
                        tokens = slice(t * P, (t + 1) * P)
                        t_.matmul(ps[:, t], gatesT[:, tokens], b2s[:], start=True, stop=False)
                        for e in range(E):
                            if t == 0 and e % 2 == 0:
                                pe.wait_ge(gated_split, st.count("ffn", 4, e // 2 + 1))
                            last = accumulate(ps[:, t], [([g[:, e, tokens] for g in gated], [w[:, e, :] for w in w2s])],
                                              first=False, final=e == E - 1)
                finish(last, name)

            def step(st):
                for h in range(H):
                    if h < 8 and st.has("late"):
                        scoresT(st, "late", h + 8)
                    if h >= 8 and st.has("score"):
                        scoresT(st, "score", h - 8)
                    if st.has("score"):
                        scores(st, h)
                    for slot, name, stage in tables(st.s)[0]:
                        if slot == h and st.has(stage):
                            work(st, name)
                    if h == 15 and st.has("proj"):
                        copied(pe, st, "values")
                    if h <= 8 and st.has("late"):
                        values_product(st, "late", h + 7)
                    if h >= 9 and st.has("score"):
                        values_product(st, "score", h - 9)

            run(pe, step)


_INS = ["x", "ctx_1024", "mask_1x1xSxS2_ik0", "L0_attn_Wq", "L0_attn_Wk", "L0_attn_Wv", "L0_xattn_wq", "L0_xattn_wk",
        "L0_xattn_wv", "L0_xattn_wo", "L0_ffn_w1", "L0_ffn_b1", "L0_ffn_w2", "L0_ffn_b2", "L0_ffn_centroids",
        "L0_ffn_w_route"]


def shape_constants():
    import numpy as np
    ident = np.eye(P, dtype=np.float32)
    onehot = np.zeros((QROWS, E, P), np.float32)
    for e in range(E):
        onehot[e, e] = 1.0
        onehot[32 + e, e] = 1.0
    inv_freq = (np.float32(1.0) / np.float32(10000.0) ** (np.arange(0, DK, 2, dtype=np.float32) / np.float32(DK)))
    angle = np.arange(S, dtype=np.float32)[None, :] * np.concatenate([inv_freq, inv_freq])[:, None].astype(np.float32)
    sign = np.where(np.arange(DK) % 2 == 0, -1.0, 1.0).astype(np.float32)[:, None]
    cos = np.tile(np.cos(angle).astype(np.float32), (HC, 1))
    sin = np.tile(np.sin(angle).astype(np.float32) * sign, (HC, 1))
    return {"c_ident": ident, "c_onehot": onehot.reshape(QROWS, E * P), "c_cos": cos, "c_sin": sin}


def kernel(**inputs):
    import numpy as np
    import concourse.bacc as bacc
    from concourse import mybir as _mybir
    from concourse.bass_utils import run_bass_kernel_spmd

    nc = bacc.Bacc("TRN2", target_bir_lowering=False, num_devices=1)
    arrays, args = {}, []
    for name in _INS:
        a = np.ascontiguousarray(inputs[name])
        arrays[f"in_{name}"] = a
        args.append(nc.dram_tensor(f"in_{name}", a.shape, _mybir.dt.from_np(a.dtype), kind="ExternalInput").ap())
    for name, a in shape_constants().items():
        arrays[name] = np.ascontiguousarray(a)
        args.append(nc.dram_tensor(name, a.shape, _mybir.dt.from_np(a.dtype), kind="ExternalInput").ap())
    args.append(nc.dram_tensor("out_dram", (B, S, D), F32, kind="ExternalOutput").ap())
    decoder_layer(nc, *args)
    r = run_bass_kernel_spmd(nc, [arrays], core_ids=[0])
    return r.results[0]["out_dram"]
```
